# Optimizing a Trainium2 kernel written in Bass

```python
import numpy as np
import jax
import jax.numpy as jnp

def _softmax(x, axis=-1):
    return jax.nn.softmax(x, axis=axis)

def _gelu(x):
    return jax.nn.gelu(x, approximate=True)

def _silu(x):
    return jax.nn.silu(x)

def _sigmoid(x):
    return jax.nn.sigmoid(x)

def _layernorm(x, axis=-1, eps=1e-05):
    m = jnp.mean(x, axis=axis, keepdims=True)
    v = jnp.var(x, axis=axis, keepdims=True)
    return (x - m) / jnp.sqrt(v + eps)

def _scatter_add(tgt, idx, src, axis=0):
    return tgt.at[idx].add(src)

def _segment_sum(src, seg, n):
    return jax.ops.segment_sum(src, seg, n)
kernel_name = 'mk_macaron_d1_jaxref_r8_2745a8'

def setup_inputs(seed: int=0):
    np.random.seed(seed)
    _w = jnp.asarray

    def _L0_attn_setup():
        import jax, jax.numpy as jnp
        import numpy as np
        import math
        HIDDEN = 256
        NUM_HEADS = 16
        HEAD_SIZE = HIDDEN // NUM_HEADS
        BATCH = 2
        SEQ = 256
        key = jax.random.key(seed)
        k_x, k_wq, k_bq, k_wo, k_bo = jax.random.split(key, 5)
        scale_in = 1.0 / math.sqrt(HIDDEN)
        return {'x': jax.random.normal(k_x, (BATCH, SEQ, HIDDEN), dtype=jnp.float32), 'Wqkv': jax.random.normal(k_wq, (HIDDEN, 3 * HIDDEN), dtype=jnp.float32) * scale_in, 'bqkv': jax.random.normal(k_bq, (3 * HIDDEN,), dtype=jnp.float32) * 0.01, 'Wo': jax.random.normal(k_wo, (HIDDEN, HIDDEN), dtype=jnp.float32) * scale_in, 'bo': jax.random.normal(k_bo, (HIDDEN,), dtype=jnp.float32) * 0.01}
    _L0_attn_in = _L0_attn_setup()

    def _L0_ffn_setup():
        import jax, jax.numpy as jnp
        import numpy as np
        HIDDEN = 256
        N_EXPERTS = 8
        N_SHARED = 2
        TOP_K = 2
        MOE_FF = 176
        SHARED_FF = N_SHARED * MOE_FF
        SCALE = 2.5
        BATCH, SEQ = (2, 128)
        key = jax.random.key(seed)
        ks = jax.random.split(key, 8)
        s = 0.02
        return {'hidden_states': jax.random.normal(ks[0], (BATCH, SEQ, HIDDEN), jnp.float32), 'gate_w': jax.random.normal(ks[1], (N_EXPERTS, HIDDEN), jnp.float32) * s, 'shared_wg': jax.random.normal(ks[2], (SHARED_FF, HIDDEN), jnp.float32) * s, 'shared_wu': jax.random.normal(ks[3], (SHARED_FF, HIDDEN), jnp.float32) * s, 'shared_wd': jax.random.normal(ks[4], (HIDDEN, SHARED_FF), jnp.float32) * s, 'exp_wg': jax.random.normal(ks[5], (N_EXPERTS, MOE_FF, HIDDEN), jnp.float32) * s, 'exp_wu': jax.random.normal(ks[6], (N_EXPERTS, MOE_FF, HIDDEN), jnp.float32) * s, 'exp_wd': jax.random.normal(ks[7], (N_EXPERTS, HIDDEN, MOE_FF), jnp.float32) * s}
    _L0_ffn_in = _L0_ffn_setup()
    _d = {'L0_attn_x': _L0_attn_in['x'], 'L0_attn_Wqkv': _L0_attn_in['Wqkv'], 'L0_attn_bqkv': _L0_attn_in['bqkv'], 'L0_attn_Wo': _L0_attn_in['Wo'], 'L0_attn_bo': _L0_attn_in['bo'], 'L0_ffn_gate_w': _L0_ffn_in['gate_w'], 'L0_ffn_shared_wg': _L0_ffn_in['shared_wg'], 'L0_ffn_shared_wu': _L0_ffn_in['shared_wu'], 'L0_ffn_shared_wd': _L0_ffn_in['shared_wd'], 'L0_ffn_exp_wg': _L0_ffn_in['exp_wg'], 'L0_ffn_exp_wu': _L0_ffn_in['exp_wu'], 'L0_ffn_exp_wd': _L0_ffn_in['exp_wd']}
    _x0 = _d['L0_attn_x']
    _d['L0_attn_x'] = jax.random.normal(jax.random.fold_in(jax.random.key(seed), 1), (4, 512, 256), dtype=_x0.dtype)
    del _x0
    return _d

def reference(L0_attn_x, L0_attn_Wqkv, L0_attn_bqkv, L0_attn_Wo, L0_attn_bo, L0_ffn_gate_w, L0_ffn_shared_wg, L0_ffn_shared_wu, L0_ffn_shared_wd, L0_ffn_exp_wg, L0_ffn_exp_wu, L0_ffn_exp_wd):

    def _L0_attn_ref(x, Wqkv, bqkv, Wo, bo):
        import jax, jax.numpy as jnp
        import numpy as np
        import math
        HIDDEN = 256
        NUM_HEADS = 16
        HEAD_SIZE = HIDDEN // NUM_HEADS
        BATCH = 2
        SEQ = 256
        b, s, _ = x.shape
        kqv = x @ Wqkv + bqkv
        kqv = kqv.reshape(b, s, 3, NUM_HEADS, HEAD_SIZE)
        q = kqv[:, :, 0]
        k = kqv[:, :, 1]
        v = kqv[:, :, 2]
        scores = jnp.einsum('bsnh,btnh->bnst', k, q) / math.sqrt(HEAD_SIZE)
        ones = jnp.ones_like(scores)
        scores = jnp.triu(scores) + -10000.0 * jnp.tril(ones, k=-1)
        attn = jax.nn.softmax(scores, axis=2)
        out = jnp.einsum('bnkq,bknh->bqnh', attn, v)
        out = out.reshape(b, s, NUM_HEADS * HEAD_SIZE)
        return out @ Wo + bo

    def _L0_ffn_ref(hidden_states, gate_w, shared_wg, shared_wu, shared_wd, exp_wg, exp_wu, exp_wd):
        import jax, jax.numpy as jnp
        import numpy as np
        HIDDEN = 256
        N_EXPERTS = 8
        N_SHARED = 2
        TOP_K = 2
        MOE_FF = 176
        SHARED_FF = N_SHARED * MOE_FF
        SCALE = 2.5
        BATCH, SEQ = (2, 128)
        B, S, D = hidden_states.shape
        T = B * S
        xf = hidden_states.reshape(T, D)
        scores = jax.nn.sigmoid(xf @ gate_w.T)
        topk_w, topk_idx = jax.lax.top_k(scores, TOP_K)
        topk_w = topk_w / (topk_w.sum(axis=-1, keepdims=True) + 1e-20)
        topk_w = topk_w * SCALE
        shared_out = jax.nn.silu(xf @ shared_wg.T) * (xf @ shared_wu.T) @ shared_wd.T
        h = jax.nn.silu(jnp.einsum('td,efd->etf', xf, exp_wg)) * jnp.einsum('td,efd->etf', xf, exp_wu)
        all_out = jnp.einsum('etf,edf->etd', h, exp_wd)
        picked = all_out[topk_idx, jnp.arange(T)[:, None]]
        routed_out = (topk_w[..., None] * picked).sum(axis=1)
        return (shared_out + routed_out).reshape(B, S, D)
    x = L0_attn_x
    x = x + 0.5 * _L0_ffn_ref(_layernorm(x, axis=-1), L0_ffn_gate_w, L0_ffn_shared_wg, L0_ffn_shared_wu, L0_ffn_shared_wd, L0_ffn_exp_wg, L0_ffn_exp_wu, L0_ffn_exp_wd)
    x = x + _L0_attn_ref(_layernorm(x, axis=-1), L0_attn_Wqkv, L0_attn_bqkv, L0_attn_Wo, L0_attn_bo)
    x = x + 0.5 * _L0_ffn_ref(_layernorm(x, axis=-1), L0_ffn_gate_w, L0_ffn_shared_wg, L0_ffn_shared_wu, L0_ffn_shared_wd, L0_ffn_exp_wg, L0_ffn_exp_wu, L0_ffn_exp_wd)
    return x

_drawn_inputs = setup_inputs


def setup_inputs(seed=0):
    import zlib

    import numpy as np

    out = dict(_drawn_inputs(seed))
    spreads = {}
    factors = {'L0_attn_bqkv': 4.878,
     'L0_attn_bo': 5.872,
     'L0_ffn_gate_w': 8.569,
     'L0_ffn_shared_wg': 2.893,
     'L0_ffn_shared_wu': 2.862,
     'L0_ffn_shared_wd': 2.857,
     'L0_ffn_exp_wg': 2.721,
     'L0_ffn_exp_wu': 2.692,
     'L0_ffn_exp_wd': 2.679}
    for name, (base, spread) in spreads.items():
        noise = np.random.default_rng([zlib.crc32(name.encode()), seed]).standard_normal(out[name].shape)
        drawn = base * np.exp(spread * noise) if base else spread * noise
        out[name] = jnp.asarray(drawn.astype(out[name].dtype))
    for name, factor in factors.items():
        out[name] = (out[name] * factor).astype(out[name].dtype)
    return out
```

```python
from contextlib import ExitStack

import numpy as np
import concourse.bass as bass
from concourse import mybir

F32 = mybir.dt.float32
F32R = mybir.dt.float32r
BF16 = mybir.dt.bfloat16
U32 = mybir.dt.uint32
I32 = mybir.dt.int32
ALU = mybir.AluOpType
ACT = mybir.ActivationFunctionType
X = mybir.AxisListType.X

P = 128
B, S, D = 4, 512, 256
T = B * S
NT = T // P
TB = S // P
KC = D // P
H, HD = 16, 16
E, FF, SF = 8, 176, 352
HC = 2
SC = 3
EPS = 1e-5
BIG = 1e30
MAX_TILES = (2 * T + E * (P - 1)) // P
NP = (MAX_TILES + 1) // 2
ROWS = NP * 2 * P

W_GATE = 0
W_SGU = W_GATE + KC * E
W_SD = W_SGU + KC * 2 * SF
W_QKV = W_SD + SC * D
W_O = W_QKV + KC * 3 * D
W_END = W_O + KC * D
EW_D = KC * 2 * FF
EW = EW_D + HC * D
STAGE = 1536

C_ID, C_U, C_ONE, C_MASK, C_IOTA = 0, P, 2 * P, 3 * P, 4 * P
C_THR = C_IOTA + NT * E
C_TRI = C_THR + E * NT
C_J = C_TRI + E * E
C_END = C_J + 2 * NP * E


def resident_chunks():
    return [(W_GATE, W_SD), (W_SD, W_QKV), (W_QKV, W_O), (W_O, W_END)]


def score_units(per):
    return [list(range(h0 + odd, h0 + 2 * per, 2)) for h0 in range(0, H, 2 * per) for odd in range(2)]


def build(nc, x_in, w_res, w_exp, bias_qkv, bias_o, consts, out):
    sorted_x = nc.dram_tensor("sorted_x", (ROWS, D), F32, kind="Internal").ap()
    sorted_y = nc.dram_tensor("sorted_y", (ROWS, D), F32, kind="Internal").ap()

    with ExitStack() as ctx:
        def sem(name):
            return ctx.enter_context(nc.semaphore(name))

        def sb(name, shape, dt, where=ctx):
            return where.enter_context(nc.sbuf_tensor(name, shape, dt))

        x = sb("x", [P, NT, D], F32)
        wh = sb("wh", [P, W_END], F32R)
        wl = sb("wl", [P, W_END], F32R)
        cst = sb("cst", [P, C_END], F32)
        tri_bf = sb("tri_bf", [P, P], BF16)
        one_bf = sb("one_bf", [P, P], BF16)
        id_bf = sb("id_bf", [P, P], BF16)
        mask_bf = sb("mask_bf", [P, P], BF16)
        stats = sb("stats", [P, NT, 6], F32)
        mv = sb("mv", [P, NT, 2], F32)
        ve = sb("ve", [P, NT], F32)
        rstd = sb("rstd", [P, NT], F32)
        nt1 = sb("nt1", [P, NT], F32)
        nt2 = sb("nt2", [P, NT], F32)
        ident = cst[:, C_ID:C_ID + P]
        banks = ctx.enter_context(nc.psum_tensor("banks", [P, 8, 512], F32))

        ffn_ctx = ExitStack()
        eh = sb("eh", [P, E, EW], F32R, ffn_ctx)
        el = sb("el", [P, E, EW], F32R, ffn_ctx)
        stage = [sb(f"stage{n}", [P, STAGE], F32, ffn_ctx) for n in range(2)]
        xn = sb("xn", [P, NT, D], F32, ffn_ctx)
        zeros = sb("zeros", [P, D], F32, ffn_ctx)
        route = {}
        for name, shape, dt in (
                ("lg", [P, NT, E], F32), ("c", [P, NT, E], F32), ("oh1", [P, NT, E], F32), ("oh2", [P, NT, E], F32),
                ("m1", [P, NT], F32), ("m2", [P, NT], F32), ("i1", [P, NT], F32),
                ("w1", [P, NT], F32), ("w2", [P, NT], F32), ("den", [P, NT], F32),
                ("cnt", [P, E, NT], F32), ("te", [P, E], F32), ("ee", [P, E, E], F32), ("inc", [P, E], F32),
                ("rk", [P, NT + 1, E], F32), ("sl1", [P, NT], F32), ("sl2", [P, NT], F32),
                ("tb", [1, 2 * NP, E], F32), ("tf", [1, 2 * NP], F32)):
            route[name] = sb("r_" + name, shape, dt, ffn_ctx)
        pick_bf = sb("pick_bf", [P, NT + 1, E], BF16, ffn_ctx)
        slot1 = sb("slot1", [P, NT], U32, ffn_ctx)
        slot2 = sb("slot2", [P, NT], U32, ffn_ctx)
        tile_expert = sb("tile_expert", [1, 2 * NP], I32, ffn_ctx)
        s_ctx = ExitStack()
        xth = sb("xth", [P, NT, KC, P], F32R, s_ctx)
        xtl = sb("xtl", [P, NT, KC, P], F32R, s_ctx)
        sg = sb("sg", [P, SF], F32, s_ctx)
        sh = sb("sh", [P, SC * P], F32, s_ctx)
        shh = sb("shh", [P, SC * P], F32R, s_ctx)
        shl = sb("shl", [P, SC * P], F32R, s_ctx)
        s_ctx.close()
        e_ctx = ExitStack()
        xs = [sb(f"xs{n}", [P, 2, D], F32, e_ctx) for n in range(2)]
        exh = [sb(f"exh{n}", [P, 2, KC, P], F32R, e_ctx) for n in range(2)]
        exl = [sb(f"exl{n}", [P, 2, KC, P], F32R, e_ctx) for n in range(2)]
        eg = sb("eg", [P, 2, FF], F32, e_ctx)
        ehid = sb("ehid", [P, 2, HC * P], F32, e_ctx)
        ehh = sb("ehh", [P, 2, HC, P], F32R, e_ctx)
        ehl = sb("ehl", [P, 2, HC, P], F32R, e_ctx)
        ys = [sb(f"ys{n}", [P, 2, D], F32, e_ctx) for n in range(2)]
        picked = [[sb(f"picked{k}_{n}", [P, D], F32, e_ctx) for k in range(2)] for n in range(4)]
        e_ctx.close()
        ffn_ctx.close()

        a_ctx = ExitStack()
        bqkv = sb("bqkv", [P, 3 * D], F32, a_ctx)
        bo = sb("bo", [P, D], F32, a_ctx)
        xa = [sb(f"xa{n}", [P, D], F32, a_ctx) for n in range(2)]
        xah = sb("xah", [P, KC, P], F32R, a_ctx)
        xal = sb("xal", [P, KC, P], F32R, a_ctx)
        qk = sb("qk", [P, 2, H, HD], F32, a_ctx)
        stack = sb("stack", [P, 2, H, 64], F32R, a_ctx)
        kT = [sb(f"kT{n}", [P, H // 2, S], F32R, a_ctx) for n in range(2)]
        q0T = sb("q0T", [P, H // 2, P], F32R, a_ctx)
        qT = [sb(f"qT{n}", [P, H // 2, P], F32R, a_ctx) for n in range(2)]
        v = [sb(f"v{n}", [P, TB, H, 32], F32, a_ctx) for n in range(2)]
        smax = sb("smax", [P, H], F32, a_ctx)
        NPR = 6
        prob = [sb(f"prob{n}", [P, 512], F32, a_ctx) for n in range(NPR)]
        oT = sb("oT", [P, TB, P], F32, a_ctx)
        rden = sb("rden", [P, H], F32, a_ctx)
        ot = sb("ot", [P, H, HD], F32, a_ctx)
        oh = sb("oh", [P, KC, P], F32R, a_ctx)
        ol = sb("ol", [P, KC, P], F32R, a_ctx)
        a_ctx.close()

        cst_in, bias_in, zeroed, zero_set = (sem(n) for n in ("cst_in", "bias_in", "zeroed", "zero_set"))
        x_in_s = [sem(f"x_in_s{b}") for b in range(B)]
        stored = sem("stored")
        cst_bf = sem("cst_bf")
        chain = sem("chain")
        staged = [sem("staged0"), sem("staged1")]
        split_hi = sem("split_hi")
        split_lo = sem("split_lo")

        FS = []
        for f in range(2):
            FS.append({n: sem(f"{n}_{f}") for n in (
                "var", "sd", "xn", "xt_ps", "xt_hi", "xt_lo", "logits", "lg_sb", "picks", "ranks", "slots",
                "sig_in", "sig", "sgu", "ssilu", "shid", "sht_ps", "sht_hi", "sht_lo", "sy", "sx",
                "scattered", "ext_ps", "ext_hi", "ext_lo", "egu", "esilu", "ehid", "eht_ps", "eht_hi",
                "eht_lo", "ey", "ey_sb", "combined")})
            for n in ("xs_in", "y_out"):
                FS[f][n] = [sem(f"{n}{par}_{f}") for par in range(2)]
            FS[f]["pick_in"] = [sem(f"pick_in{n}_{f}") for n in range(4)]
        AS = {n: sem("a_" + n) for n in (
            "var", "sd", "xn", "xt_ps", "xt_hi", "xt_lo", "qkv", "qk_sb", "v_sb", "hi", "lo", "dup",
            "kt_ps", "kt_sb", "q0_ps", "q0_sb", "s1", "mx", "m_st", "qt_ps", "qt_sb", "s2", "p", "av", "ot_ps_in",
            "o_ps", "o_sb", "oc_ps", "oc_hi", "oc_lo", "y", "done", "mem", "tri", "bo", "m_hi")}

        block = ctx.enter_context(nc.Block())
        links = [0]

        pieces = []
        for a, b in resident_chunks():
            pieces.append((w_res[:, a:b], wh[:, a:b], wl[:, a:b]))
        N_RES = len(pieces)
        for f in range(2):
            for e in range(E):
                pieces.append((w_exp[:, e, :], eh[:, e, :], el[:, e, :]))

        def piece_dma(eng, n):
            src, hi, _ = pieces[n]
            if n >= 2:
                eng.wait_ge(split_lo, n - 1)
            eng.dma_start(stage[n % 2][:, 0:hi.shape[1]], src).then_inc(staged[n % 2], 16)

        def piece_hi(n):
            _, hi, _ = pieces[n]
            nc.scalar.wait_ge(staged[n % 2], 16 * (n // 2 + 1))
            nc.scalar.activation(hi, stage[n % 2][:, 0:hi.shape[1]], ACT.Copy).then_inc(split_hi, 1)

        def piece_lo(n):
            _, hi, lo = pieces[n]
            nc.gpsimd.wait_ge(split_hi, n + 1)
            nc.gpsimd.tensor_tensor(lo, stage[n % 2][:, 0:hi.shape[1]], hi.bitcast(F32), ALU.subtract)\
                .then_inc(split_lo, 1)

        def exact3(pe, out_ap, xhi, xlo, whi, wlo, first, last):
            pe.matmul(out_ap, xhi, whi, start=first, stop=False)
            pe.matmul(out_ap, xhi, wlo, start=False, stop=False)
            return pe.matmul(out_ap, xlo, whi, start=False, stop=last)

        @block.sync
        def _(sp):
            sp.dma_start(cst[:], consts).then_inc(cst_in, 16)
            for b in range(B):
                sp.dma_start(x[:, TB * b:TB * b + TB, :],
                             x_in[b].rearrange("(i p) d -> p i d", p=P)).then_inc(x_in_s[b], 16)
            for n in range(N_RES):
                piece_dma(sp, n)
            sp.wait_ge(zero_set, 1)
            sp.dma_start(sorted_x.rearrange("(r q) d -> q r d", q=P),
                         zeros[:].unsqueeze(1).to_broadcast([P, 2 * NP, D])).then_inc(zeroed, 16)
            for f in range(2):
                s = FS[f]
                if f == 1:
                    sp.wait_ge(AS["done"], NT)
                for e in range(E):
                    piece_dma(sp, N_RES + f * E + e)
                sp.wait_ge(s["scattered"], 32 * NT)

                def load(p, par):
                    sp.dma_start(xs[par][:], sorted_x[bass.ds(p * (2 * P), 2 * P), :]
                                 .rearrange("(c q) d -> q c d", q=P)).then_inc(s["xs_in"][par], 16)

                def store(p, par):
                    sp.wait_ge(s["ey_sb"], p + 1)
                    sp.dma_start(sorted_y[bass.ds(p * (2 * P), 2 * P), :]
                                 .rearrange("(c q) d -> q c d", q=P), ys[par][:]).then_inc(s["y_out"][par], 16)

                sp.wait_ge(s["sy"], NT)
                sp.wait_ge(s["sx"], NT)
                load(0, 0)
                load(1, 1)
                with sp.Fori(0, NP // 2 - 1) as m:
                    i = 2 * m
                    for par in range(2):
                        sp.wait_ge(s["ext_ps"], i + par + 1)
                        load(i + par + 2, par)
                        store(i + par, par)
                store(NP - 2, 0)
                store(NP - 1, 1)
                if f == 0:
                    sp.wait_ge(s["combined"], NT)
                    sp.dma_start(bqkv[:], bias_qkv).then_inc(bias_in, 16)
                    sp.dma_start(bo[:], bias_o).then_inc(bias_in, 16)
                else:
                    for g in range(NT // 4):
                        sp.wait_ge(s["combined"], 4 * g + 4)
                        sp.dma_start(out[g].rearrange("(i p) d -> p i d", p=P), x[:, 4 * g:4 * g + 4, :])\
                            .then_inc(stored, 16)
                    sp.wait_ge(stored, 16 * (NT // 4))

        def attention_pool(pool):
            s = AS
            pool.wait_ge(FS[0]["combined"], NT)
            nc.gpsimd.memset(stack[:, 0, :, 48:64].bitcast(F32), 0.0).then_inc(s["mem"], 1)
            nc.gpsimd.memset(stack[:, 1, :, 48:50].bitcast(F32), 1.0).then_inc(s["mem"], 1)
            nc.gpsimd.memset(stack[:, 1, :, 50:64].bitcast(F32), 0.0).then_inc(s["mem"], 1)
            for n in range(2):
                nc.gpsimd.memset(v[n][:, :, :, 16:17], 1.0).then_inc(s["mem"], 1)
                nc.gpsimd.memset(v[n][:, :, :, 17:32], 0.0).then_inc(s["mem"], 1)
            pool.wait_ge(bias_in, 32)
            for i in range(NT):
                pool.wait_ge(s["hi"], i + 1)
                if i >= 1:
                    pool.wait_ge(s["qt_ps"], i)
                nc.gpsimd.tensor_copy(stack[:, 0, :, 32:48], stack[:, 0, :, 0:16].bitcast(F32)).then_inc(s["dup"], 1)
                nc.gpsimd.tensor_copy(stack[:, 1, :, 16:32], stack[:, 1, :, 0:16].bitcast(F32)).then_inc(s["dup"], 1)
                pool.wait_ge(s["xn"], i + 1)
                nc.gpsimd.tensor_tensor(x[:, i, :], x[:, i, :], bo[:], ALU.add).then_inc(s["bo"], 1)

        @block.gpsimd
        def _(pool):
            nc.gpsimd.memset(zeros[:], 0.0).then_inc(zero_set, 1)
            for n in range(N_RES):
                piece_lo(n)
            for f in range(2):
                s = FS[f]
                if f == 0:
                    pool.wait_ge(zeroed, 16)
                pool.wait_ge(s["slots"], 2)
                pool.wait_ge(s["xn"], NT)
                for i in range(NT):
                    for slot in (slot1, slot2):
                        pool.indirect_dma_start(
                            out=sorted_x, out_offset=bass.IndirectOffsetOnAxis(ap=slot[:, i:i + 1], axis=0),
                            in_=xn[:, i, :], in_offset=None).then_inc(s["scattered"], 16)
                for e in range(E):
                    piece_lo(N_RES + f * E + e)
                for par in range(2):
                    pool.wait_ge(s["y_out"][par], 16 * (NP // 2))
                for i in range(NT):
                    if i >= 4:
                        pool.wait_ge(s["combined"], i - 3)
                    for k, slot in enumerate((slot1, slot2)):
                        pool.indirect_dma_start(
                            out=picked[i % 4][k][:], out_offset=None, in_=sorted_y,
                            in_offset=bass.IndirectOffsetOnAxis(ap=slot[:, i:i + 1], axis=0))\
                            .then_inc(s["pick_in"][i % 4], 16)
                if f == 0:
                    attention_pool(pool)

        def attention_scalar(act):
            s = AS
            act.wait_ge(s["var"], 1)
            nc.scalar.activation(rstd[:], ve[:], ACT.Sqrt).then_inc(s["sd"], 1)
            act.wait_ge(s["mem"], 7)
            unit2 = 0
            for i in range(NT):
                b, j = divmod(i, TB)
                act.wait_ge(s["xt_ps"], i + 1)
                nc.scalar.activation(xah[:], banks[:, 0, 0:D].rearrange("p (k t) -> p k t", k=KC), ACT.Copy)\
                    .then_inc(s["xt_hi"], 1)
                act.wait_ge(s["qk_sb"], i + 1)
                if i >= 1:
                    act.wait_ge(s["qt_ps"], i)
                nc.scalar.activation(stack[:, :, :, 0:16], qk[:], ACT.Copy).then_inc(s["hi"], 1)
                act.wait_ge(s["kt_ps"], i + 1)
                nc.scalar.activation(kT[b % 2][:, :, j * P:j * P + P],
                                     banks[:, 1:3, :].rearrange("p a (g t) -> p (a g) t", g=4), ACT.Copy)\
                    .then_inc(s["kt_sb"], 1)
                act.wait_ge(s["q0_ps"], i + 1)
                nc.scalar.activation(q0T[:], banks[:, 1:3, :].rearrange("p a (g t) -> p (a g) t", g=4), ACT.Copy)\
                    .then_inc(s["q0_sb"], 1)
                act.wait_ge(s["qt_ps"], i + 1)
                nc.scalar.activation(qT[i % 2][:], banks[:, 1:3, :].rearrange("p a (g t) -> p (a g) t", g=4), ACT.Copy)\
                    .then_inc(s["qt_sb"], 1)
                n = (j + 1) * P
                for h in range(H):
                    u = i * H + h
                    act.wait_ge(s["s2"], u + 1)
                    if u >= NPR:
                        act.wait_ge(s["av"], (u - NPR) // 4 + 1)
                    nc.scalar.activation(prob[u % NPR][:, 0:n], banks[:, 5 + u % 2, 0:n], ACT.Exp, scale=HD ** -0.5)\
                        .then_inc(s["p"], 1)
                act.wait_ge(s["av"], 4 * (i + 1))
                nc.scalar.activation(oT[:], banks[:, 7, :].rearrange("p (g t) -> p g t", g=4), ACT.Copy)\
                    .then_inc(s["ot_ps_in"], 1)
                act.wait_ge(s["oc_ps"], i + 1)
                nc.scalar.activation(oh[:], banks[:, 0, 0:D].rearrange("p (k t) -> p k t", k=KC), ACT.Copy)\
                    .then_inc(s["oc_hi"], 1)

        @block.scalar
        def _(act):
            for n in range(N_RES):
                piece_hi(n)
            for f in range(2):
                s = FS[f]
                act.wait_ge(s["var"], 1)
                nc.scalar.activation(rstd[:], ve[:], ACT.Sqrt).then_inc(s["sd"], 1)
                for q in range(NT // 2):
                    act.wait_ge(s["xt_ps"], q + 1)
                    nc.scalar.activation(xth[:, 2 * q:2 * q + 2, :, :], banks[:, q % 2, :]
                                         .rearrange("p (c k t) -> p c k t", c=2, k=KC), ACT.Copy).then_inc(s["xt_hi"], 1)
                act.wait_ge(s["sig_in"], 2)
                for m in ("m1", "m2"):
                    nc.scalar.activation(route["w" + m[1]][:], route[m][:], ACT.Sigmoid).then_inc(s["sig"], 1)
                for i in range(NT):
                    act.wait_ge(s["sgu"], i + 1)
                    if i >= 1:
                        act.wait_ge(s["shid"], i)
                    nc.scalar.activation(sg[:], banks[:, 3, 0:SF], ACT.Silu).then_inc(s["ssilu"], 1)
                    act.wait_ge(s["sht_ps"], i + 1)
                    if i >= 1:
                        act.wait_ge(s["sy"], i)
                    nc.scalar.activation(shh[:], banks[:, 5, 0:SC * P], ACT.Copy).then_inc(s["sht_hi"], 1)
                    if i % 2 == 1:
                        piece_hi(N_RES + f * E + i // 2)

                def silu(p):
                    act.wait_ge(s["egu"], p + 1)
                    nc.scalar.activation(eg[:], banks[:, 3:5, 0:FF], ACT.Silu).then_inc(s["esilu"], 1)

                def x_hi(p, par):
                    act.wait_ge(s["ext_ps"], p + 1)
                    nc.scalar.activation(exh[par][:], banks[:, 0, :].rearrange("p (c k t) -> p c k t", c=2, k=KC),
                                         ACT.Copy).then_inc(s["ext_hi"], 1)

                def h_hi(p):
                    act.wait_ge(s["eht_ps"], p + 1)
                    nc.scalar.activation(ehh[:], banks[:, 5, :].rearrange("p (c k t) -> p c k t", c=2, k=HC),
                                         ACT.Copy).then_inc(s["eht_hi"], 1)

                x_hi(0, 0)
                with act.Fori(0, NP // 2 - 1) as m:
                    i = 2 * m
                    for par in range(2):
                        x_hi(i + par + 1, 1 - par)
                        silu(i + par)
                        h_hi(i + par)
                x_hi(NP - 1, 1)
                silu(NP - 2)
                h_hi(NP - 2)
                silu(NP - 1)
                h_hi(NP - 1)
                if f == 0:
                    attention_scalar(act)

        def attention_tensor(pe):
            s = AS
            unit1 = 0
            for i in range(NT):
                b, j = divmod(i, TB)
                n = (j + 1) * P
                pe.wait_ge(s["xn"], i + 1)
                if i >= 1:
                    pe.wait_ge(s["done"], i)
                for k in range(KC):
                    mm = pe.transpose(banks[:, 0, k * P:k * P + P], xa[i % 2][:, k * P:k * P + P], ident)
                mm.then_inc(s["xt_ps"], 1)
                pe.wait_ge(s["xt_lo"], i + 1)
                if i == 0:
                    pe.wait_ge(split_lo, N_RES)
                if i >= 1:
                    pe.wait_ge(s["qt_sb"], i)
                for k in range(KC):
                    at = W_QKV + k * 3 * D
                    exact3(pe, banks[:, 1, 0:2 * D], xah[:, k, :], xal[:, k, :], wh[:, at:at + 2 * D],
                           wl[:, at:at + 2 * D], k == 0, k == KC - 1)
                    mm = exact3(pe, banks[:, 2, 0:D], xah[:, k, :], xal[:, k, :], wh[:, at + 2 * D:at + 3 * D],
                                wl[:, at + 2 * D:at + 3 * D], k == 0, k == KC - 1)
                mm.then_inc(s["qkv"], 1)

                def turn_stack(which, done):
                    for g in range(H // 2):
                        m = pe.transpose(banks[:, 1 + g // 4, (g % 4) * P:(g % 4) * P + P],
                                         stack[:, which, 2 * g:2 * g + 2, :].rearrange("p a b -> p (a b)").bitcast(F32),
                                         ident)
                    m.then_inc(s[done], 1)

                pe.wait_ge(s["v_sb"], i + 1)
                pe.wait_ge(s["lo"], 2 * i + 2)
                pe.wait_ge(s["dup"], 2 * i + 2)
                turn_stack(1, "kt_ps")
                pe.wait_ge(s["kt_sb"], i + 1)
                turn_stack(0, "q0_ps")
                pe.wait_ge(s["q0_sb"], i + 1)
                per = 512 // n
                for heads in score_units(per):
                    if unit1 >= 2:
                        pe.wait_ge(s["mx"], unit1 - 1)
                    for a, h in enumerate(heads):
                        r = 64 * (h % 2)
                        o = banks[:, 3 + unit1 % 2, a * n:a * n + n]
                        pe.matmul(o, q0T[r:r + 48, h // 2, :], kT[b % 2][r:r + 48, h // 2, 0:n], start=True, stop=True)
                        mm = pe.matmul(o[:, n - P:n], id_bf[:], mask_bf[:], start=False, stop=True,
                                       skip_group_check=True)
                    mm.then_inc(s["s1"], 1)
                    unit1 += 1
                pe.wait_ge(s["m_hi"], 2 * i + 2)
                turn_stack(0, "qt_ps")
                pe.wait_ge(s["qt_sb"], i + 1)

                def weigh(g):
                    pe.wait_ge(s["p"], i * H + 4 * g + 4)
                    if g == 0 and i >= 1:
                        pe.wait_ge(s["ot_ps_in"], i)
                    for t in range(j + 1):
                        for c in range(4):
                            h = 4 * g + c
                            m = pe.matmul(banks[32 * c:32 * c + 32, 7, g * P:g * P + P], v[b % 2][:, t, h, :],
                                          prob[(i * H + h) % NPR][:, t * P:t * P + P], start=t == 0, stop=t == j)
                    m.then_inc(s["av"], 1)

                for h in range(H):
                    u = i * H + h
                    if u >= 2:
                        pe.wait_ge(s["p"], u - 1)
                    r = 64 * (h % 2)
                    for t in range(j + 1):
                        mm = pe.matmul(banks[:, 5 + u % 2, t * P:t * P + P], kT[b % 2][r:r + 50, h // 2, t * P:t * P + P],
                                       qT[i % 2][r:r + 50, h // 2, :], start=True, stop=True)
                    mm = pe.matmul(banks[:, 5 + u % 2, j * P:j * P + P], mask_bf[:], id_bf[:], start=False, stop=True,
                                   skip_group_check=True)
                    mm.then_inc(s["s2"], 1)
                    if h % 4 == 1 and h > 4:
                        weigh(h // 4 - 1)
                weigh(3)
                pe.wait_ge(s["ot_ps_in"], i + 1)
                for g in range(4):
                    mm = pe.transpose(banks[:, 0, g * P:g * P + P], oT[:, g, :], ident)
                mm.then_inc(s["o_ps"], 1)
                pe.wait_ge(s["o_sb"], i + 1)
                for k in range(KC):
                    mm = pe.transpose(banks[:, 0, k * P:k * P + P],
                                      ot[:].rearrange("p h d -> p (h d)")[:, k * P:k * P + P], ident)
                mm.then_inc(s["oc_ps"], 1)
                pe.wait_ge(s["oc_lo"], i + 1)
                for k in range(KC):
                    at = W_O + k * D
                    mm = exact3(pe, banks[:, 0, 0:D], oh[:, k, :], ol[:, k, :], wh[:, at:at + D], wl[:, at:at + D],
                                k == 0, k == KC - 1)
                mm.then_inc(s["y"], 1)

        @block.tensor
        def _(pe):
            pe.wait_ge(cst_in, 16)
            pe.wait_ge(cst_bf, 4)
            for f in range(2):
                s = FS[f]
                logits = banks[:, 2, 0:NT * E].rearrange("p (i e) -> p i e", e=E)

                def router(q):
                    pe.wait_ge(s["xt_lo"], q + 1)
                    if q == 0:
                        pe.wait_ge(split_lo, 1)
                    for i in (2 * q, 2 * q + 1):
                        for k in range(KC):
                            g = slice(W_GATE + k * E, W_GATE + k * E + E)
                            mm = exact3(pe, logits[:, i, :], xth[:, i, k, :], xtl[:, i, k, :], wh[:, g], wl[:, g],
                                        k == 0, k == KC - 1)
                    if q == NT // 2 - 1:
                        mm.then_inc(s["logits"], 1)

                for q in range(NT // 2):
                    pe.wait_ge(s["xn"], 2 * q + 2)
                    if q >= 2:
                        pe.wait_ge(s["xt_lo"], q - 1)
                    for c in range(2):
                        for k in range(KC):
                            at = (c * KC + k) * P
                            mm = pe.transpose(banks[:, q % 2, at:at + P], xn[:, 2 * q + c, k * P:k * P + P], ident)
                    mm.then_inc(s["xt_ps"], 1)
                    if q >= 1:
                        router(q - 1)
                router(NT // 2 - 1)

                def s_up(i):
                    if i >= 1:
                        pe.wait_ge(s["shid"], i)
                    for k in range(KC):
                        for half in range(2):
                            at = W_SGU + (k * 2 + half) * SF
                            mm = exact3(pe, banks[:, 3 + half, 0:SF], xth[:, i, k, :], xtl[:, i, k, :],
                                        wh[:, at:at + SF], wl[:, at:at + SF], k == 0, k == KC - 1)
                    mm.then_inc(s["sgu"], 1)

                def s_turn(i):
                    pe.wait_ge(s["shid"], i + 1)
                    if i >= 1:
                        pe.wait_ge(s["sht_lo"], i)
                    for c in range(SC):
                        mm = pe.transpose(banks[:, 5, c * P:c * P + P], sh[:, c * P:c * P + P], ident)
                    mm.then_inc(s["sht_ps"], 1)

                def s_down(i):
                    pe.wait_ge(s["sht_lo"], i + 1)
                    if i == 0:
                        pe.wait_ge(split_lo, 2)
                    if i >= 2:
                        pe.wait_ge(s["sx"], i - 1)
                    for c in range(SC):
                        at = W_SD + c * D
                        mm = exact3(pe, banks[:, 6 + i % 2, 0:D], shh[:, c * P:c * P + P], shl[:, c * P:c * P + P],
                                    wh[:, at:at + D], wl[:, at:at + D], c == 0, c == SC - 1)
                    mm.then_inc(s["sy"], 1)

                s_up(0)
                pe.wait_ge(s["picks"], 1)
                ranks = banks[:, 2, 0:(NT + 1) * E].rearrange("p (i e) -> p i e", e=E)
                pe.matmul(ranks, tri_bf[:], pick_bf[:], start=True, stop=False)
                for i in range(NT):
                    mm = pe.matmul(ranks[:, i + 1:NT + 1, :], one_bf[:],
                                   pick_bf[:, i:i + 1, :].to_broadcast([P, NT - i, E]),
                                   start=False, stop=i == NT - 1)
                mm.then_inc(s["ranks"], 1)
                s_turn(0)
                for i in range(1, NT):
                    s_up(i)
                    s_down(i - 1)
                    s_turn(i)
                s_down(NT - 1)

                eh2 = eh[:].rearrange("p e w -> p (e w)")
                el2 = el[:].rearrange("p e w -> p (e w)")

                def turn(p, par, loads):
                    pe.wait_ge(s["xs_in"][par], loads * 16)
                    if not (isinstance(p, int) and p == 0):
                        pe.wait_ge(s["ext_lo"], p)
                    for c in range(2):
                        for k in range(KC):
                            at = (c * KC + k) * P
                            mm = pe.transpose(banks[:, 0, at:at + P], xs[par][:, c, k * P:k * P + P], ident)
                    mm.then_inc(s["ext_ps"], 1)

                def experts_of(p):
                    return [pe.value_load(tile_expert[0:1, bass.ds(2 * p + c, 1)], min_val=0, max_val=E - 1)
                            for c in range(2)]

                def up(p, par, which):
                    pe.wait_ge(s["ext_lo"], p + 1)
                    for c in range(2):
                        e = which[c]
                        for k in range(KC):
                            w, n = k * 2 * FF, 2 * FF
                            mm = exact3(pe, banks[:, 3 + c, 0:2 * FF], exh[par][:, c, k, :], exl[par][:, c, k, :],
                                        eh2[:, bass.ds(e * EW + w, n)], el2[:, bass.ds(e * EW + w, n)], k == 0, k == KC - 1)
                    mm.then_inc(s["egu"], 1)

                def h_turn(p):
                    pe.wait_ge(s["ehid"], p + 1)
                    for c in range(2):
                        for k in range(HC):
                            at = (c * HC + k) * P
                            mm = pe.transpose(banks[:, 5, at:at + P], ehid[:, c, k * P:k * P + P], ident)
                    mm.then_inc(s["eht_ps"], 1)

                def down(p, par, which):
                    pe.wait_ge(s["eht_lo"], p + 1)
                    for c in range(2):
                        e = which[c]
                        for k in range(HC):
                            w, n = EW_D + k * D, D
                            mm = exact3(pe, banks[:, 6 + par, c * D:(c + 1) * D], ehh[:, c, k, :], ehl[:, c, k, :],
                                        eh2[:, bass.ds(e * EW + w, n)], el2[:, bass.ds(e * EW + w, n)], k == 0, k == HC - 1)
                    mm.then_inc(s["ey"], 1)

                pe.wait_ge(s["slots"], 3)
                pe.wait_ge(split_lo, N_RES + (f + 1) * E)
                turn(0, 0, 1)
                turn(1, 1, 1)
                up(0, 0, experts_of(0))
                h_turn(0)
                with pe.Fori(0, NP // 2 - 1) as m:
                    i = 2 * m + 1
                    for d, par in ((0, 1), (1, 0)):
                        here, before = experts_of(i + d), experts_of(i + d - 1)
                        turn(i + d + 1, 1 - par, m + 2)
                        up(i + d, par, here)
                        down(i + d - 1, 1 - par, before)
                        h_turn(i + d)
                here, before = experts_of(NP - 1), experts_of(NP - 2)
                up(NP - 1, 1, here)
                down(NP - 2, 0, before)
                h_turn(NP - 1)
                down(NP - 1, 1, here)
                if f == 0:
                    attention_tensor(pe)

        def attention_vector(dve, link, norm_stats):
            s = AS
            norm_stats(s, None)
            dve.wait_ge(bias_in, 32)
            unit1 = 0
            for i in range(NT):
                b, j = divmod(i, TB)
                n = (j + 1) * P
                nc.vector.tensor_scalar(xa[i % 2][:], x[:, i, :], mv[:, i, 0:1], rstd[:, i:i + 1],
                                        ALU.subtract, ALU.mult).then_inc(s["xn"], 1)
                dve.wait_ge(s["xt_hi"], i + 1)
                nc.vector.tensor_tensor(xal[:], banks[:, 0, 0:D].rearrange("p (k t) -> p k t", k=KC),
                                        xah[:].bitcast(F32), ALU.subtract).then_inc(s["xt_lo"], 1)
                dve.wait_ge(s["qkv"], i + 1)
                nc.vector.tensor_tensor(qk[:], banks[:, 1, :].rearrange("p (a h d) -> p a h d", a=2, h=H),
                                        bqkv[:, 0:2 * D].rearrange("p (a h d) -> p a h d", a=2, h=H), ALU.add)\
                    .then_inc(s["qk_sb"], 1)
                if i == 0:
                    dve.wait_ge(s["mem"], 7)
                nc.vector.tensor_tensor(v[b % 2][:, j, :, 0:HD], banks[:, 2, 0:D].rearrange("p (h d) -> p h d", h=H),
                                        bqkv[:, 2 * D:3 * D].rearrange("p (h d) -> p h d", h=H), ALU.add)\
                    .then_inc(s["v_sb"], 1)
                dve.wait_ge(s["hi"], i + 1)
                nc.vector.tensor_tensor(stack[:, 0, :, 16:32], qk[:, 0, :, :], stack[:, 0, :, 0:16].bitcast(F32),
                                        ALU.subtract).then_inc(s["lo"], 1)
                nc.vector.tensor_tensor(stack[:, 1, :, 32:48], qk[:, 1, :, :], stack[:, 1, :, 0:16].bitcast(F32),
                                        ALU.subtract).then_inc(s["lo"], 1)
                per = 512 // n
                for heads in score_units(per):
                    dve.wait_ge(s["s1"], unit1 + 1)
                    nc.vector.tensor_reduce(smax[:, heads[0]:heads[-1] + 1:2],
                                            banks[:, 3 + unit1 % 2, 0:per * n].rearrange("p (h s) -> p h s", h=per),
                                            X, ALU.max).then_inc(s["mx"], 1)
                    unit1 += 1
                dve.wait_ge(s["mx"], unit1)
                dve.wait_ge(s["q0_ps"], i + 1)
                nc.vector.tensor_scalar(stack[:, 0, :, 48], smax[:], -1.0, None, ALU.mult).then_inc(s["m_hi"], 1)
                dve.wait_ge(s["m_hi"], 2 * i + 1)
                nc.vector.scalar_tensor_tensor(stack[:, 0, :, 49], smax[:], -1.0, stack[:, 0, :, 48].bitcast(F32),
                                               ALU.mult, ALU.subtract).then_inc(s["m_hi"], 1)
                dve.wait_ge(s["o_ps"], i + 1)
                o = banks[:, 0, :].rearrange("p (h c) -> p h c", c=32)
                link(nc.vector.reciprocal(rden[:], o[:, :, 16]))
                nc.vector.tensor_tensor(ot[:], o[:, :, 0:HD], rden[:].unsqueeze(2).to_broadcast([P, H, HD]), ALU.mult)\
                    .then_inc(s["o_sb"], 1)
                dve.wait_ge(s["oc_hi"], i + 1)
                nc.vector.tensor_tensor(ol[:], banks[:, 0, 0:D].rearrange("p (k t) -> p k t", k=KC),
                                        oh[:].bitcast(F32), ALU.subtract).then_inc(s["oc_lo"], 1)
                dve.wait_ge(s["y"], i + 1)
                dve.wait_ge(s["bo"], i + 1)
                nc.vector.tensor_tensor(x[:, i, :], banks[:, 0, 0:D], x[:, i, :], ALU.add).then_inc(s["done"], 1)
            dve.wait_ge(s["done"], NT)

        @block.vector
        def _(dve):
            def link(ins):
                links[0] += 1
                ins.then_inc(chain, 1)
                dve.wait_ge(chain, links[0])

            def norm_stats(s, loaded):
                for i in range(NT):
                    if loaded is not None and i % TB == 0:
                        dve.wait_ge(loaded[i // TB], 16)
                    ins = nc.vector.bn_stats(stats[:, i, :], x[:, i, :])
                link(ins)
                for i in range(NT):
                    ins = nc.vector.bn_aggr(mv[:, i, :], stats[:, i, :])
                link(ins)
                nc.vector.tensor_scalar(ve[:], mv[:, :, 1], EPS, None, ALU.add).then_inc(s["var"], 1)
                dve.wait_ge(s["sd"], 1)
                link(nc.vector.reciprocal(rstd[:], rstd[:]))
                link(nc.vector.tensor_tensor(nt1[:], ve[:], rstd[:], ALU.mult))
                link(nc.vector.tensor_tensor(nt2[:], nt1[:], rstd[:], ALU.mult))
                link(nc.vector.tensor_scalar(nt1[:], nt2[:], -0.5, 1.5, ALU.mult, ALU.add))
                link(nc.vector.tensor_tensor(rstd[:], rstd[:], nt1[:], ALU.mult))

            dve.wait_ge(cst_in, 16)
            for dst, at in ((tri_bf, C_U), (one_bf, C_ONE), (id_bf, C_ID), (mask_bf, C_MASK)):
                nc.vector.tensor_copy(dst[:], cst[:, at:at + P]).then_inc(cst_bf, 1)

            for f in range(2):
                s = FS[f]
                r = route
                norm_stats(s, x_in_s if f == 0 else None)
                nc.vector.memset(sh[:, SF:SC * P], 0.0)
                nc.vector.memset(pick_bf[:, NT, :], 0.0)
                for i in range(NT):
                    nc.vector.tensor_scalar(xn[:, i, :], x[:, i, :], mv[:, i, 0:1], rstd[:, i:i + 1],
                                            ALU.subtract, ALU.mult).then_inc(s["xn"], 1)
                for q in range(NT // 2):
                    dve.wait_ge(s["xt_hi"], q + 1)
                    nc.vector.tensor_tensor(xtl[:, 2 * q:2 * q + 2, :, :],
                                            banks[:, q % 2, :].rearrange("p (c k t) -> p c k t", c=2, k=KC),
                                            xth[:, 2 * q:2 * q + 2, :, :].bitcast(F32), ALU.subtract)\
                        .then_inc(s["xt_lo"], 1)
                iota = cst[:, C_IOTA:C_IOTA + NT * E].rearrange("p (i e) -> p i e", e=E)

                def wide(ap):
                    return ap[:].unsqueeze(2).to_broadcast([P, NT, E])

                dve.wait_ge(s["logits"], 1)
                link(nc.vector.tensor_copy(r["lg"][:], banks[:, 2, 0:NT * E].rearrange("p (i e) -> p i e", e=E)))
                for m, hot in (("m1", "oh1"), ("m2", "oh2")):
                    ins = nc.vector.tensor_reduce(r[m][:], r["lg"][:], X, ALU.max)
                    ins.then_inc(s["sig_in"], 1)
                    dve.wait_ge(s["sig_in"], 1 if m == "m1" else 2)
                    link(nc.vector.tensor_tensor(r["c"][:], r["lg"][:], wide(r[m]), ALU.is_equal))
                    link(nc.vector.scalar_tensor_tensor(r["c"][:], r["c"][:], -float(E), iota, ALU.mult, ALU.add))
                    link(nc.vector.tensor_reduce(r["i1"][:], r["c"][:], X, ALU.min))
                    link(nc.vector.tensor_scalar(r["i1"][:], r["i1"][:], float(E), None, ALU.add))
                    link(nc.vector.tensor_tensor(r[hot][:], iota, wide(r["i1"]), ALU.is_equal))
                    if m == "m1":
                        link(nc.vector.scalar_tensor_tensor(r["lg"][:], r[hot][:], -BIG, r["lg"][:], ALU.mult, ALU.add))
                nc.vector.tensor_tensor(pick_bf[:, 0:NT, :], r["oh1"][:], r["oh2"][:], ALU.add).then_inc(s["picks"], 1)
                dve.wait_ge(s["sig"], 2)
                link(nc.vector.scalar_tensor_tensor(r["den"][:], r["w1"][:], 1e-20, r["w2"][:], ALU.add, ALU.add))
                link(nc.vector.reciprocal(r["den"][:], r["den"][:]))
                link(nc.vector.scalar_tensor_tensor(r["w1"][:], r["w1"][:], 1.25, r["den"][:], ALU.mult, ALU.mult))
                link(nc.vector.scalar_tensor_tensor(r["w2"][:], r["w2"][:], 1.25, r["den"][:], ALU.mult, ALU.mult))
                dve.wait_ge(s["ranks"], 1)
                link(nc.vector.tensor_copy(r["rk"][:], banks[:, 2, 0:(NT + 1) * E].rearrange("p (i e) -> p i e", e=E)))
                link(nc.vector.tensor_tensor(r["cnt"][:], r["rk"][:, NT, :].unsqueeze(2).to_broadcast([P, E, NT]),
                                             cst[:, C_THR:C_THR + E * NT].rearrange("p (e j) -> p e j", e=E), ALU.is_gt))
                link(nc.vector.tensor_reduce(r["te"][:], r["cnt"][:], X, ALU.add))
                link(nc.vector.tensor_tensor(r["ee"][:], cst[:, C_TRI:C_TRI + E * E].rearrange("p (a b) -> p a b", a=E),
                                             r["te"][:].unsqueeze(1).to_broadcast([P, E, E]), ALU.mult))
                link(nc.vector.tensor_reduce(r["inc"][:], r["ee"][:], X, ALU.add))
                link(nc.vector.tensor_tensor(r["te"][:], r["inc"][:], r["te"][:], ALU.subtract))
                link(nc.vector.scalar_tensor_tensor(r["rk"][:, 0:NT, :], r["te"][:].unsqueeze(1).to_broadcast([P, NT, E]),
                                                    float(P), r["rk"][:, 0:NT, :], ALU.mult, ALU.add))
                for hot, sl, slot in (("oh1", "sl1", slot1), ("oh2", "sl2", slot2)):
                    link(nc.vector.tensor_tensor(r["c"][:], r[hot][:], r["rk"][:, 0:NT, :], ALU.mult))
                    link(nc.vector.tensor_reduce(r[sl][:], r["c"][:], X, ALU.add))
                    nc.vector.tensor_copy(slot[:], r[sl][:]).then_inc(s["slots"], 1)
                link(nc.vector.tensor_tensor(r["tb"][:], r["inc"][0:1, :].unsqueeze(1).to_broadcast([1, 2 * NP, E]),
                                             cst[0:1, C_J:C_J + 2 * NP * E].rearrange("p (j e) -> p j e", e=E),
                                             ALU.is_le))
                link(nc.vector.tensor_reduce(r["tf"][:], r["tb"][:], X, ALU.add))
                link(nc.vector.tensor_scalar(r["tf"][:], r["tf"][:], float(E - 1), None, ALU.min))
                nc.vector.tensor_copy(tile_expert[:], r["tf"][:]).then_inc(s["slots"], 1)
                def s_out(i):
                    dve.wait_ge(s["sy"], i + 1)
                    nc.vector.scalar_tensor_tensor(x[:, i, :], banks[:, 6 + i % 2, 0:D], 0.5, x[:, i, :],
                                                   ALU.mult, ALU.add).then_inc(s["sx"], 1)

                for i in range(NT):
                    dve.wait_ge(s["ssilu"], i + 1)
                    if i >= 1:
                        dve.wait_ge(s["sht_ps"], i)
                    nc.vector.tensor_tensor(sh[:, 0:SF], sg[:], banks[:, 4, 0:SF], ALU.mult).then_inc(s["shid"], 1)
                    if i >= 1:
                        s_out(i - 1)
                    dve.wait_ge(s["sht_hi"], i + 1)
                    nc.vector.tensor_tensor(shl[:], banks[:, 5, 0:SC * P], shh[:].bitcast(F32), ALU.subtract)\
                        .then_inc(s["sht_lo"], 1)
                s_out(NT - 1)

                link(nc.vector.memset(ehid[:], 0.0))

                def x_lo(p, par):
                    dve.wait_ge(s["ext_hi"], p + 1)
                    nc.vector.tensor_tensor(exl[par][:], banks[:, 0, :].rearrange("p (c k t) -> p c k t", c=2, k=KC),
                                            exh[par][:].bitcast(F32), ALU.subtract).then_inc(s["ext_lo"], 1)

                def hidden(p):
                    dve.wait_ge(s["esilu"], p + 1)
                    nc.vector.tensor_tensor(ehid[:, :, 0:FF], eg[:], banks[:, 3:5, FF:2 * FF], ALU.mult)\
                        .then_inc(s["ehid"], 1)

                def h_lo(p):
                    dve.wait_ge(s["eht_hi"], p + 1)
                    nc.vector.tensor_tensor(ehl[:], banks[:, 5, :].rearrange("p (c k t) -> p c k t", c=2, k=HC),
                                            ehh[:].bitcast(F32), ALU.subtract).then_inc(s["eht_lo"], 1)

                def y_out(p, par, stores):
                    dve.wait_ge(s["ey"], p + 1)
                    if stores is not None:
                        dve.wait_ge(s["y_out"][par], stores * 16)
                    nc.vector.tensor_copy(ys[par][:], banks[:, 6 + par, :].rearrange("p (c d) -> p c d", c=2))\
                        .then_inc(s["ey_sb"], 1)

                x_lo(0, 0)
                x_lo(1, 1)
                hidden(0)
                h_lo(0)
                x_lo(2, 0)
                hidden(1)
                y_out(0, 0, None)
                h_lo(1)
                x_lo(3, 1)
                hidden(2)
                y_out(1, 1, None)
                h_lo(2)
                with dve.Fori(0, NP // 2 - 2) as m:
                    i = 2 * m + 3
                    for d, par in ((0, 1), (1, 0)):
                        x_lo(i + d + 1, 1 - par)
                        hidden(i + d)
                        y_out(i + d - 1, 1 - par, m + 1)
                        h_lo(i + d)
                hidden(NP - 1)
                y_out(NP - 2, 0, NP // 2 - 1)
                h_lo(NP - 1)
                y_out(NP - 1, 1, NP // 2 - 1)
                for i in range(NT):
                    dve.wait_ge(s["pick_in"][i % 4], 32 * (i // 4 + 1))
                    link(nc.vector.scalar_tensor_tensor(x[:, i, :], picked[i % 4][0][:], r["w1"][:, i:i + 1],
                                                        x[:, i, :], ALU.mult, ALU.add))
                    nc.vector.scalar_tensor_tensor(x[:, i, :], picked[i % 4][1][:], r["w2"][:, i:i + 1],
                                                   x[:, i, :], ALU.mult, ALU.add).then_inc(s["combined"], 1)
                if f == 0:
                    dve.wait_ge(s["combined"], NT)
                    attention_vector(dve, link, norm_stats)


def constants():
    c = np.zeros((P, C_END), np.float32)
    r = np.arange(P)
    c[:, C_ID:C_ID + P] = np.eye(P)
    c[:, C_U:C_U + P] = r[:, None] < r[None, :]
    c[:, C_ONE:C_ONE + P] = 1.0
    c[:, C_MASK:C_MASK + P] = np.where(r[None, :] > r[:, None], -BIG, 0.0)
    c[:, C_IOTA:C_IOTA + NT * E] = np.tile(np.arange(E), NT)
    c[:, C_THR:C_THR + E * NT] = np.tile(P * np.arange(NT), E)
    c[:, C_TRI:C_TRI + E * E] = (np.arange(E)[None, :] <= np.arange(E)[:, None]).reshape(-1)
    c[:, C_J:C_J + 2 * NP * E] = np.repeat(np.arange(2 * NP), E)
    return c


def rows_by_chunk(w):
    k = w.shape[0] // P
    return w.reshape(k, P, -1).transpose(1, 0, 2).reshape(P, -1)


def padded(w, rows):
    return np.concatenate([w, np.zeros((rows - w.shape[0], w.shape[1]), w.dtype)])


def kernel(**inputs):
    import concourse.bacc as bacc
    from concourse.bass_utils import run_bass_kernel_spmd as run

    a = {k.replace("L0_", ""): np.asarray(v) for k, v in inputs.items()}
    resident = np.concatenate([
        rows_by_chunk(a["ffn_gate_w"].T),
        rows_by_chunk(np.concatenate([a["ffn_shared_wg"], a["ffn_shared_wu"]]).T),
        rows_by_chunk(padded(a["ffn_shared_wd"].T, SC * P)),
        rows_by_chunk(a["attn_Wqkv"]),
        rows_by_chunk(a["attn_Wo"])], axis=1)
    experts = np.stack([np.concatenate([
        rows_by_chunk(np.concatenate([a["ffn_exp_wg"][e], a["ffn_exp_wu"][e]]).T),
        rows_by_chunk(padded(a["ffn_exp_wd"][e].T, HC * P))], axis=1) for e in range(E)], axis=1)
    arrays = {
        "x_in": a["attn_x"], "w_res": resident, "w_exp": experts,
        "bias_qkv": np.broadcast_to(a["attn_bqkv"], (P, 3 * D)), "bias_o": np.broadcast_to(a["attn_bo"], (P, D)),
        "consts": constants()}
    arrays = {k: np.ascontiguousarray(v) for k, v in arrays.items()}
    nc = bacc.Bacc("TRN2", target_bir_lowering=False, num_devices=1)
    aps = [nc.dram_tensor(k, v.shape, F32, kind="ExternalInput").ap() for k, v in arrays.items()]
    out = nc.dram_tensor("out", (B, S, D), F32, kind="ExternalOutput").ap()
    build(nc, *aps, out)
    return run(nc, [arrays], core_ids=[0]).results[0]["out"]
```

```python
from contextlib import ExitStack

import numpy as np
import concourse.bass as bass
from concourse import mybir

F32 = mybir.dt.float32
F32R = mybir.dt.float32r
BF16 = mybir.dt.bfloat16
U32 = mybir.dt.uint32
I32 = mybir.dt.int32
ALU = mybir.AluOpType
ACT = mybir.ActivationFunctionType
X = mybir.AxisListType.X

P = 128
B, S, D = 4, 512, 256
T = B * S
NT = T // P
TB = S // P
KC = D // P
H, HD = 16, 16
E, FF, SF = 8, 176, 352
HC = 2
SC = 3
EPS = 1e-5
BIG = 1e30
MAX_TILES = (2 * T + E * (P - 1)) // P
NP = (MAX_TILES + 1) // 2
ROWS = NP * 2 * P

W_GATE = 0
W_SGU = W_GATE + KC * E
W_SD = W_SGU + KC * 2 * SF
W_QKV = W_SD + SC * D
W_O = W_QKV + KC * 3 * D
W_END = W_O + KC * D
EW_D = KC * 2 * FF
EW = EW_D + HC * D
STAGE = 1536

C_ID, C_U, C_ONE, C_MASK, C_IOTA = 0, P, 2 * P, 3 * P, 4 * P
C_THR = C_IOTA + NT * E
C_TRI = C_THR + E * NT
C_J = C_TRI + E * E
C_END = C_J + 2 * NP * E


def resident_chunks():
    return [(W_GATE, W_SGU), (W_SGU, W_SD), (W_SD, W_QKV), (W_QKV, W_O), (W_O, W_END)]


def bound_units(i):
    per = TB // (i % TB + 1)
    return [list(range(h, h + per)) for h in range(0, H, per)]


def score_units(i):
    blocks = [(pair, t) for pair in range(H // 2) for t in range(i % TB + 1)]
    return [blocks[n:n + 2] for n in range(0, len(blocks), 2)]


def units_at(n, step, steps):
    return [u for u in range(n) if u * steps // n == step]


def build(nc, x_in, w_res, w_exp, bias_qkv, bias_o, consts, out):
    sorted_x = nc.dram_tensor("sorted_x", (ROWS, D), F32, kind="Internal").ap()
    sorted_y = nc.dram_tensor("sorted_y", (ROWS, D), F32, kind="Internal").ap()

    with ExitStack() as ctx:
        def sem(name):
            return ctx.enter_context(nc.semaphore(name))

        def sb(name, shape, dt, where=ctx):
            return where.enter_context(nc.sbuf_tensor(name, shape, dt))

        x = sb("x", [P, NT, D], F32)
        wh = sb("wh", [P, W_END], F32R)
        wl = sb("wl", [P, W_END], F32R)
        cst = sb("cst", [P, C_END], F32)
        tri_bf = sb("tri_bf", [P, P], BF16)
        one_bf = sb("one_bf", [P, P], BF16)
        id_r = sb("id_r", [P, P], F32R)
        id_bf = sb("id_bf", [P, P], BF16)
        mask_bf = sb("mask_bf", [P, P], BF16)
        stats = sb("stats", [P, NT, 6], F32)
        mv = sb("mv", [P, NT, 2], F32)
        ve = sb("ve", [P, NT], F32)
        rstd = sb("rstd", [P, NT], F32)
        nt1 = sb("nt1", [P, NT], F32)
        nt2 = sb("nt2", [P, NT], F32)
        ident = cst[:, C_ID:C_ID + P]
        banks = ctx.enter_context(nc.psum_tensor("banks", [P, 8, 512], F32))

        ffn_ctx = ExitStack()
        eh = sb("eh", [P, E, EW], F32R, ffn_ctx)
        el = sb("el", [P, E, EW], F32R, ffn_ctx)
        stage = [sb(f"stage{n}", [P, STAGE], F32, ffn_ctx) for n in range(2)]
        xn = sb("xn", [P, NT, D], F32, ffn_ctx)
        zeros = sb("zeros", [P, D], F32, ffn_ctx)
        route = {}
        for name, shape, dt in (
                ("lg", [P, NT, E], F32), ("c", [P, NT, E], F32), ("oh1", [P, NT, E], F32), ("oh2", [P, NT, E], F32),
                ("m1", [P, NT], F32), ("m2", [P, NT], F32), ("i1", [P, NT], F32),
                ("w1", [P, NT], F32), ("w2", [P, NT], F32), ("den", [P, NT], F32),
                ("cnt", [P, E, NT], F32), ("te", [P, E], F32), ("ee", [P, E, E], F32), ("inc", [P, E], F32),
                ("rk", [P, NT + 1, E], F32), ("sl1", [P, NT], F32), ("sl2", [P, NT], F32),
                ("tb", [1, 2 * NP, E], F32), ("tf", [1, 2 * NP], F32)):
            route[name] = sb("r_" + name, shape, dt, ffn_ctx)
        pick_bf = sb("pick_bf", [P, NT + 1, E], BF16, ffn_ctx)
        slot1 = sb("slot1", [P, NT], U32, ffn_ctx)
        slot2 = sb("slot2", [P, NT], U32, ffn_ctx)
        tile_weights = sb("tile_weights", [1, 2 * NP], I32, ffn_ctx)
        s_ctx = ExitStack()
        xth = sb("xth", [P, NT, KC, P], F32R, s_ctx)
        xtl = sb("xtl", [P, NT, KC, P], F32R, s_ctx)
        l_ctx = ExitStack()
        turned_logits = sb("turned_logits", [E, 2, 4 * P], F32, l_ctx)
        l_ctx.close()
        sg = sb("sg", [P, SF], F32, s_ctx)
        sh = sb("sh", [P, SC * P], F32, s_ctx)
        shh = sb("shh", [P, SC * P], F32R, s_ctx)
        shl = sb("shl", [P, SC * P], F32R, s_ctx)
        s_ctx.close()
        e_ctx = ExitStack()
        xs = [sb(f"xs{n}", [P, 2, D], F32, e_ctx) for n in range(4)]
        exh = [sb(f"exh{n}", [P, 2, KC, P], F32R, e_ctx) for n in range(2)]
        exl = [sb(f"exl{n}", [P, 2, KC, P], F32R, e_ctx) for n in range(2)]
        eg = sb("eg", [P, 2, FF], F32, e_ctx)
        ehid = sb("ehid", [P, 2, HC * P], F32, e_ctx)
        ehh = sb("ehh", [P, 2, HC, P], F32R, e_ctx)
        ehl = sb("ehl", [P, 2, HC, P], F32R, e_ctx)
        ys = [sb(f"ys{n}", [P, 2, D], F32, e_ctx) for n in range(2)]
        picked = [[sb(f"picked{k}_{n}", [P, D], F32, e_ctx) for k in range(2)] for n in range(4)]
        e_ctx.close()
        ffn_ctx.close()

        a_ctx = ExitStack()
        bqkv = sb("bqkv", [P, 3 * D], F32, a_ctx)
        bo = sb("bo", [P, D], F32, a_ctx)
        xa = [sb(f"xa{n}", [P, D], F32, a_ctx) for n in range(2)]
        xah = sb("xah", [P, KC, P], F32R, a_ctx)
        xal = sb("xal", [P, KC, P], F32R, a_ctx)
        qk = sb("qk", [P, 2, H, HD], F32, a_ctx)
        stack = [sb(f"stack{n}", [P, 2, H, 64], F32R, a_ctx) for n in range(2)]
        kT = [sb(f"kT{n}", [P, H // 2, S], F32R, a_ctx) for n in range(2)]
        q0T = [sb(f"q0T{n}", [P, H, P], F32R, a_ctx) for n in range(2)]
        qT = [sb(f"qT{n}", [P, H, P], F32R, a_ctx) for n in range(2)]
        v = [sb(f"v{n}", [P, TB, H, 32], F32, a_ctx) for n in range(2)]
        smax = sb("smax", [P, H], F32, a_ctx)
        NPR = 8
        prob = [sb(f"prob{n}", [P, 512], F32, a_ctx) for n in range(NPR)]
        oT = sb("oT", [P, TB, P], F32, a_ctx)
        rden = sb("rden", [P, H], F32, a_ctx)
        ot = sb("ot", [P, H, HD], F32, a_ctx)
        oh = sb("oh", [P, KC, P], F32R, a_ctx)
        ol = sb("ol", [P, KC, P], F32R, a_ctx)
        a_ctx.close()

        cst_in, bias_in, zeroed, zero_set = (sem(n) for n in ("cst_in", "bias_in", "zeroed", "zero_set"))
        x_in_s = [sem(f"x_in_s{b}") for b in range(B)]
        stored = sem("stored")
        cst_bf = sem("cst_bf")
        chain = sem("chain")
        row_stats_in = sem("row_stats_in")
        staged = [sem("staged0"), sem("staged1")]
        split_hi = sem("split_hi")
        split_res = sem("split_res")
        split_exp = sem("split_exp")

        FS = []
        for f in range(2):
            FS.append({n: sem(f"{n}_{f}") for n in (
                "var", "sd", "xn", "xt_ps", "xt_hi", "xt_lo", "lt_ps", "lt_sb", "logits", "picks", "ranks", "slots",
                "sig_in", "sig", "sgu", "ssilu", "shid", "sht_ps", "sht_hi", "sht_lo", "sy", "sx",
                "scattered", "ext_ps", "ext_hi", "ext_lo", "egu", "esilu", "ehid", "eht_ps", "eht_hi",
                "eht_lo", "ey", "ey_sb", "combined")})
            FS[f]["y_out"] = [sem(f"y_out{n}_{f}") for n in range(2)]
            for name in ("xs_in", "pick_in"):
                FS[f][name] = [sem(f"{name}{n}_{f}") for n in range(4)]
        AS = {n: sem("a_" + n) for n in (
            "var", "sd", "xn", "xt_ps", "xt_hi", "xt_lo", "qkv", "qk_sb", "v_sb", "hi", "lo", "dup",
            "kt_ps", "kt_sb", "q0_ps", "q0_even", "q0_odd", "s1", "mx", "qt_ps", "qt_even", "qt_odd",
            "clear", "s2", "p", "av", "ot_ps_in",
            "o_ps", "o_sb", "oc_ps", "oc_hi", "oc_lo", "y", "done", "mem", "tri", "bo", "m_hi")}

        block = ctx.enter_context(nc.Block())
        links = [0]
        bound_base = [sum(len(bound_units(t)) for t in range(i)) for i in range(NT + 1)]
        score_base = [sum(len(score_units(t)) for t in range(i)) for i in range(NT + 1)]

        pieces = []
        for a, b in resident_chunks():
            pieces.append((w_res[:, a:b], wh[:, a:b], wl[:, a:b]))
        N_RES = len(pieces)
        for f in range(2):
            for e in range(E):
                pieces.append((w_exp[:, e, :], eh[:, e, :], el[:, e, :]))

        def piece_dma(eng, n):
            src, hi, _ = pieces[n]
            if n >= 2:
                if n - 2 < N_RES:
                    eng.wait_ge(split_res, n - 1)
                else:
                    eng.wait_ge(split_exp, n - 1 - N_RES)
            eng.dma_start(stage[n % 2][:, 0:hi.shape[1]], src).then_inc(staged[n % 2], 16)

        def piece_hi(n):
            _, hi, _ = pieces[n]
            nc.scalar.wait_ge(staged[n % 2], 16 * (n // 2 + 1))
            nc.scalar.activation(hi, stage[n % 2][:, 0:hi.shape[1]], ACT.Copy).then_inc(split_hi, 1)

        def piece_lo(eng, n):
            _, hi, lo = pieces[n]
            eng.tensor_tensor(lo, stage[n % 2][:, 0:hi.shape[1]], hi.bitcast(F32), ALU.subtract)\
                .then_inc(split_res if n < N_RES else split_exp, 1)

        def exact3(pe, out_ap, xhi, xlo, whi, wlo, first, last):
            pe.matmul(out_ap, xhi, whi, start=first, stop=False)
            pe.matmul(out_ap, xhi, wlo, start=False, stop=False)
            return pe.matmul(out_ap, xlo, whi, start=False, stop=last)

        @block.sync
        def _(sp):
            for b in range(B):
                sp.dma_start(x[:, TB * b:TB * b + TB, :],
                             x_in[b].rearrange("(i p) d -> p i d", p=P)).then_inc(x_in_s[b], 16)
            sp.dma_start(cst[:], consts).then_inc(cst_in, 16)
            for n in range(N_RES):
                piece_dma(sp, n)
            sp.wait_ge(zero_set, 1)
            sp.dma_start(sorted_x.rearrange("(r q) d -> q r d", q=P),
                         zeros[:].unsqueeze(1).to_broadcast([P, 2 * NP, D])).then_inc(zeroed, 16)
            for f in range(2):
                s = FS[f]
                if f == 1:
                    sp.wait_ge(AS["done"], NT)
                for e in range(E):
                    piece_dma(sp, N_RES + f * E + e)
                sp.wait_ge(s["scattered"], 32 * NT)

                def load(p, n):
                    sp.dma_start(xs[n][:], sorted_x[bass.ds(p * (2 * P), 2 * P), :]
                                 .rearrange("(c q) d -> q c d", q=P)).then_inc(s["xs_in"][n], 16)

                sp.wait_ge(s["sy"], NT)
                sp.wait_ge(s["sx"], NT)
                for n in range(4):
                    load(n, n)
                with sp.Fori(0, NP // 4 - 1) as m:
                    i = 4 * m
                    for n in range(4):
                        sp.wait_ge(s["ext_ps"], i + n + 1)
                        load(i + n + 4, n)
                if f == 0:
                    sp.wait_ge(s["combined"], NT)
                    sp.dma_start(bqkv[:], bias_qkv).then_inc(bias_in, 16)
                    sp.dma_start(bo[:], bias_o).then_inc(bias_in, 16)
                else:
                    for g in range(NT // 4):
                        sp.wait_ge(s["combined"], 4 * g + 4)
                        sp.dma_start(out[g].rearrange("(i p) d -> p i d", p=P), x[:, 4 * g:4 * g + 4, :])\
                            .then_inc(stored, 16)
                    sp.wait_ge(stored, 16 * (NT // 4))

        def attention_pool(pool):
            s = AS
            pool.wait_ge(FS[0]["combined"], NT)
            for n in range(2):
                nc.gpsimd.memset(stack[n][:, 0, :, 48:64].bitcast(F32), 0.0).then_inc(s["mem"], 1)
                nc.gpsimd.memset(stack[n][:, 1, :, 48:50].bitcast(F32), 1.0).then_inc(s["mem"], 1)
                nc.gpsimd.memset(stack[n][:, 1, :, 50:64].bitcast(F32), 0.0).then_inc(s["mem"], 1)
                nc.gpsimd.memset(v[n][:, :, :, 16:17], 1.0).then_inc(s["mem"], 1)
                nc.gpsimd.memset(v[n][:, :, :, 17:32], 0.0).then_inc(s["mem"], 1)
            for h in (0, H // 2):
                nc.gpsimd.memset(q0T[0][:, h:h + H // 2, :].bitcast(F32), 0.0).then_inc(s["clear"], 1)
            pool.wait_ge(bias_in, 32)
            for i in range(NT):
                st = stack[i % 2]
                pool.wait_ge(s["hi"], i + 1)
                nc.gpsimd.tensor_copy(st[:, 1, :, 16:32], st[:, 1, :, 0:16].bitcast(F32)).then_inc(s["dup"], 1)
                nc.gpsimd.tensor_copy(st[:, 0, :, 32:48], st[:, 0, :, 0:16].bitcast(F32)).then_inc(s["dup"], 1)
                pool.wait_ge(s["xn"], i + 1)
                nc.gpsimd.tensor_tensor(x[:, i, :], x[:, i, :], bo[:], ALU.add).then_inc(s["bo"], 1)

        @block.gpsimd
        def _(pool):
            nc.gpsimd.memset(zeros[:], 0.0).then_inc(zero_set, 1)
            for n in range(N_RES):
                pool.wait_ge(split_hi, n + 1)
                piece_lo(nc.gpsimd, n)
            for f in range(2):
                s = FS[f]
                if f == 0:
                    pool.wait_ge(zeroed, 16)
                pool.wait_ge(s["slots"], 2)
                pool.wait_ge(s["xn"], NT)
                for i in range(NT):
                    for slot in (slot1, slot2):
                        pool.indirect_dma_start(
                            out=sorted_x, out_offset=bass.IndirectOffsetOnAxis(ap=slot[:, i:i + 1], axis=0),
                            in_=xn[:, i, :], in_offset=None).then_inc(s["scattered"], 16)


                def store(p, par):
                    pool.wait_ge(s["ey_sb"], p + 1)
                    pool.dma_start(sorted_y[bass.ds(p * (2 * P), 2 * P), :]
                                   .rearrange("(c q) d -> q c d", q=P), ys[par][:]).then_inc(s["y_out"][par], 16)

                with pool.Fori(0, NP // 2) as m:
                    for par in range(2):
                        store(2 * m + par, par)
                for par in range(2):
                    pool.wait_ge(s["y_out"][par], 16 * (NP // 2))
                for i in range(NT):
                    if i >= 4:
                        pool.wait_ge(s["combined"], i - 3)
                    for k, slot in enumerate((slot1, slot2)):
                        pool.indirect_dma_start(
                            out=picked[i % 4][k][:], out_offset=None, in_=sorted_y,
                            in_offset=bass.IndirectOffsetOnAxis(ap=slot[:, i:i + 1], axis=0))\
                            .then_inc(s["pick_in"][i % 4], 16)
                if f == 0:
                    attention_pool(pool)

        def attention_scalar(act):
            s = AS
            act.wait_ge(s["var"], 1)
            nc.scalar.activation(rstd[:], ve[:], ACT.Sqrt).then_inc(s["sd"], 1)
            act.wait_ge(s["mem"], 10)

            def turned():
                return banks[:, 1:3, :].rearrange("p a (g t) -> p (a g) t", g=4)

            def x_hi(i):
                act.wait_ge(s["xt_ps"], i + 1)
                nc.scalar.activation(xah[:], banks[:, 0, 0:D].rearrange("p (k t) -> p k t", k=KC), ACT.Copy)\
                    .then_inc(s["xt_hi"], 1)

            def qk_hi(i):
                act.wait_ge(s["qk_sb"], i + 1)
                nc.scalar.activation(stack[i % 2][:, :, :, 0:16], qk[:], ACT.Copy).then_inc(s["hi"], 1)

            def keep_k(i):
                b, j = divmod(i, TB)
                act.wait_ge(s["kt_ps"], i + 1)
                nc.scalar.activation(kT[b % 2][:, :, j * P:j * P + P], turned(), ACT.Copy).then_inc(s["kt_sb"], 1)

            def keep_q0(i):
                act.wait_ge(s["q0_ps"], i + 1)
                if i < 2:
                    act.wait_ge(s["clear"], 2 + 4 * i)
                nc.scalar.activation(q0T[i % 2][0:48, 0:H:2, :], turned()[0:48], ACT.Copy).then_inc(s["q0_even"], 1)

            def keep_q(i):
                act.wait_ge(s["qt_ps"], i + 1)
                if i < 2:
                    act.wait_ge(s["clear"], 4 + 4 * i)
                nc.scalar.activation(qT[i % 2][0:64, 0:H:2, :], turned()[0:64], ACT.Copy).then_inc(s["qt_even"], 1)

            weighed = [4 * i + unit // (i % TB + 1) + 1 for i in range(NT) for unit in range(len(score_units(i)))]

            def exponentials(i, unit):
                u = score_base[i] + unit
                act.wait_ge(s["s2"], u + 1)
                if u >= NPR:
                    act.wait_ge(s["av"], weighed[u - NPR])
                nc.scalar.activation(prob[u % NPR][:], banks[:, 5 + u % 2, :], ACT.Exp, scale=HD ** -0.5)\
                    .then_inc(s["p"], 1)

            def keep_o(i):
                act.wait_ge(s["av"], 4 * (i + 1))
                nc.scalar.activation(oT[:], banks[:, 7, :].rearrange("p (g t) -> p g t", g=4), ACT.Copy)\
                    .then_inc(s["ot_ps_in"], 1)

            def o_hi(i):
                act.wait_ge(s["oc_ps"], i + 1)
                nc.scalar.activation(oh[:], banks[:, 0, 0:D].rearrange("p (k t) -> p k t", k=KC), ACT.Copy)\
                    .then_inc(s["oc_hi"], 1)

            after = {0: ((x_hi, 2),), 2: ((keep_o, -1),), 4: ((qk_hi, 2),), 6: ((o_hi, -1),), 8: ((keep_k, 2),),
                     11: ((keep_q0, 2),), 14: ((keep_q, 1),)}
            for i in range(-2, NT + 1):
                for step in range(16):
                    if 0 <= i < NT:
                        for unit in units_at(len(score_units(i)), step, 16):
                            exponentials(i, unit)
                    for part, ahead in after.get(step, ()):
                        if 0 <= i + ahead < NT:
                            part(i + ahead)

        @block.scalar
        def _(act):
            for f in range(2):
                s = FS[f]
                act.wait_ge(s["var"], 1)
                nc.scalar.activation(rstd[:], ve[:], ACT.Sqrt).then_inc(s["sd"], 1)
                if f == 0:
                    for n in range(3):
                        piece_hi(n)
                for q in range(NT // 2):
                    act.wait_ge(s["xt_ps"], q + 1)
                    nc.scalar.activation(xth[:, 2 * q:2 * q + 2, :, :], banks[:, q % 2, :]
                                         .rearrange("p (c k t) -> p c k t", c=2, k=KC), ACT.Copy).then_inc(s["xt_hi"], 1)
                    for g in {3: (0,), 5: (1,), 7: (2, 3)}.get(q, ()):
                        act.wait_ge(s["lt_ps"], g + 1)
                        if g >= 2:
                            act.wait_ge(s["logits"], g - 1)
                        nc.scalar.activation(turned_logits[:, g % 2, :], banks[0:E, 6 + g % 2, :], ACT.Copy)\
                            .then_inc(s["lt_sb"], 1)
                for i in range(NT):
                    act.wait_ge(s["sgu"], i + 1)
                    if i == 0:
                        act.wait_ge(s["logits"], 4)
                    else:
                        act.wait_ge(s["shid"], i)
                    nc.scalar.activation(sg[:], banks[:, 3, 0:SF], ACT.Silu).then_inc(s["ssilu"], 1)
                    act.wait_ge(s["sht_ps"], i + 1)
                    if i >= 1:
                        act.wait_ge(s["sy"], i)
                    nc.scalar.activation(shh[:], banks[:, 5, 0:SC * P], ACT.Copy).then_inc(s["sht_hi"], 1)
                    if i == 1:
                        act.wait_ge(s["sig_in"], 2)
                        for m in ("m1", "m2"):
                            nc.scalar.activation(route["w" + m[1]][:], route[m][:], ACT.Sigmoid).then_inc(s["sig"], 1)
                    if f == 0 and i in (2, 3):
                        piece_hi(i + 1)
                    if 5 <= i < 5 + E:
                        piece_hi(N_RES + f * E + i - 5)

                def silu(p):
                    act.wait_ge(s["egu"], p + 1)
                    nc.scalar.activation(eg[:], banks[:, 3:5, 0:FF], ACT.Silu).then_inc(s["esilu"], 1)

                def x_hi(p, par):
                    act.wait_ge(s["ext_ps"], p + 1)
                    nc.scalar.activation(exh[par][:], banks[:, 0, :].rearrange("p (c k t) -> p c k t", c=2, k=KC),
                                         ACT.Copy).then_inc(s["ext_hi"], 1)

                def h_hi(p):
                    act.wait_ge(s["eht_ps"], p + 1)
                    nc.scalar.activation(ehh[:], banks[:, 5, :].rearrange("p (c k t) -> p c k t", c=2, k=HC),
                                         ACT.Copy).then_inc(s["eht_hi"], 1)

                x_hi(0, 0)
                with act.Fori(0, NP // 2 - 1) as m:
                    i = 2 * m
                    for par in range(2):
                        x_hi(i + par + 1, 1 - par)
                        silu(i + par)
                        h_hi(i + par)
                x_hi(NP - 1, 1)
                silu(NP - 2)
                h_hi(NP - 2)
                silu(NP - 1)
                h_hi(NP - 1)
                if f == 0:
                    attention_scalar(act)

        def attention_tensor(pe):
            s = AS

            def x_turn(i):
                pe.wait_ge(s["xn"], i + 1)
                if i >= 4:
                    pe.wait_ge(s["done"], i - 3)
                elif i >= 1:
                    pe.wait_ge(s["xt_lo"], i)
                for k in range(KC):
                    mm = pe.transpose(banks[:, 0, k * P:k * P + P], xa[i % 2][:, k * P:k * P + P], ident)
                mm.then_inc(s["xt_ps"], 1)

            def project(i):
                pe.wait_ge(s["xt_lo"], i + 1)
                if i == 0:
                    pe.wait_ge(split_res, N_RES)
                if i >= 2:
                    pe.wait_ge(s["qt_even"], i - 1)
                    pe.wait_ge(s["qt_odd"], i - 1)
                elif i == 1:
                    pe.wait_ge(s["q0_even"], 1)
                    pe.wait_ge(s["q0_odd"], 1)
                for k in range(KC):
                    at = W_QKV + k * 3 * D
                    exact3(pe, banks[:, 1, 0:2 * D], xah[:, k, :], xal[:, k, :], wh[:, at:at + 2 * D],
                           wl[:, at:at + 2 * D], k == 0, k == KC - 1)
                    mm = exact3(pe, banks[:, 2, 0:D], xah[:, k, :], xal[:, k, :], wh[:, at + 2 * D:at + 3 * D],
                                wl[:, at + 2 * D:at + 3 * D], k == 0, k == KC - 1)
                mm.then_inc(s["qkv"], 1)

            def turn_stack(i, which, done):
                for g in range(H // 2):
                    mm = pe.matmul(banks[:, 1 + g // 4, (g % 4) * P:(g % 4) * P + P],
                                   stack[i % 2][:, which, 2 * g:2 * g + 2, :].rearrange("p a b -> p (a b)"),
                                   id_r[:], start=True, stop=True)
                mm.then_inc(s[done], 1)

            def k_turn(i):
                pe.wait_ge(s["v_sb"], i + 1)
                pe.wait_ge(s["lo"], 2 * i + 2)
                pe.wait_ge(s["dup"], 2 * i + 2)
                turn_stack(i, 1, "kt_ps")

            def q0_turn(i):
                pe.wait_ge(s["kt_sb"], i + 1)
                turn_stack(i, 0, "q0_ps")

            def q_turn(i):
                pe.wait_ge(s["m_hi"], 2 * i + 2)
                if i + 1 < NT:
                    pe.wait_ge(s["q0_even"], i + 2)
                    pe.wait_ge(s["q0_odd"], i + 2)
                turn_stack(i, 0, "qt_ps")

            def bound(i, unit):
                b, j = divmod(i, TB)
                n = (j + 1) * P
                u = bound_base[i] + unit
                heads = bound_units(i)[unit]
                if unit == 0:
                    pe.wait_ge(s["q0_even"], i + 1)
                    pe.wait_ge(s["q0_odd"], i + 1)
                if u >= 2:
                    pe.wait_ge(s["mx"], u - 1)
                o = banks[:, 3 + u % 2, 0:len(heads) * n].rearrange("p (h s) -> p h s", s=n)
                for a, h in enumerate(heads):
                    pe.matmul(o[:, a, :], q0T[i % 2][:, h, :], kT[b % 2][:, h // 2, 0:n], start=True, stop=True)
                pe.matmul(o[:, :, n - P:n], id_bf[:], mask_bf[:].unsqueeze(1).to_broadcast([P, len(heads), P]),
                          start=False, stop=True, skip_group_check=True).then_inc(s["s1"], 1)

            def scores(i, unit):
                b, j = divmod(i, TB)
                u = score_base[i] + unit
                if unit == 0:
                    pe.wait_ge(s["qt_even"], i + 1)
                    pe.wait_ge(s["qt_odd"], i + 1)
                if u >= 2:
                    pe.wait_ge(s["p"], u - 1)
                for a, (pair, t) in enumerate(score_units(i)[unit]):
                    o = banks[:, 5 + u % 2, a * 2 * P:(a + 1) * 2 * P].rearrange("p (h s) -> p h s", h=2)
                    mm = pe.matmul(o, kT[b % 2][:, pair, t * P:t * P + P], qT[i % 2][:, 2 * pair:2 * pair + 2, :],
                                   start=True, stop=True)
                    if t == j:
                        mm = pe.matmul(o, mask_bf[:], id_bf[:].unsqueeze(1).to_broadcast([P, 2, P]),
                                       start=False, stop=True, skip_group_check=True)
                mm.then_inc(s["s2"], 1)

            def weigh(i, g):
                b, j = divmod(i, TB)
                pe.wait_ge(s["p"], score_base[i] + (g + 1) * (j + 1))
                if g == 0 and i >= 1:
                    pe.wait_ge(s["ot_ps_in"], i)
                for t in range(j + 1):
                    for c in range(4):
                        h = 4 * g + c
                        unit, half = divmod(h // 2 * (j + 1) + t, 2)
                        at = (2 * half + h % 2) * P
                        mm = pe.matmul(banks[32 * c:32 * c + 32, 7, g * P:g * P + P], v[b % 2][:, t, h, :],
                                       prob[(score_base[i] + unit) % NPR][:, at:at + P], start=t == 0, stop=t == j)
                mm.then_inc(s["av"], 1)

            def o_turn(i):
                pe.wait_ge(s["ot_ps_in"], i + 1)
                if i + 3 < NT:
                    pe.wait_ge(s["xt_lo"], i + 4)
                else:
                    pe.wait_ge(s["done"], i)
                for g in range(4):
                    mm = pe.transpose(banks[:, 0, g * P:g * P + P], oT[:, g, :], ident)
                mm.then_inc(s["o_ps"], 1)

            def oc_turn(i):
                pe.wait_ge(s["o_sb"], i + 1)
                for k in range(KC):
                    mm = pe.transpose(banks[:, 0, k * P:k * P + P],
                                      ot[:].rearrange("p h d -> p (h d)")[:, k * P:k * P + P], ident)
                mm.then_inc(s["oc_ps"], 1)

            def out_project(i):
                pe.wait_ge(s["oc_lo"], i + 1)
                for k in range(KC):
                    at = W_O + k * D
                    mm = exact3(pe, banks[:, 0, 0:D], oh[:, k, :], ol[:, k, :], wh[:, at:at + D], wl[:, at:at + D],
                                k == 0, k == KC - 1)
                mm.then_inc(s["y"], 1)

            before = {0: ((x_turn, 2),), 2: ((project, 2),), 3: ((o_turn, -1),), 5: ((oc_turn, -1),),
                      7: ((k_turn, 2),), 8: ((out_project, -1),), 10: ((q0_turn, 2),), 13: ((q_turn, 1),)}
            for i in range(-2, NT + 1):
                for step in range(16):
                    for part, ahead in before.get(step, ()):
                        if 0 <= i + ahead < NT:
                            part(i + ahead)
                    if 0 <= i < NT:
                        for unit in units_at(len(score_units(i)), step, 16):
                            scores(i, unit)
                    if 0 <= i + 1 < NT:
                        for unit in units_at(len(bound_units(i + 1)), step, 11):
                            bound(i + 1, unit)
                    if step == 1 and 0 <= i - 1 < NT:
                        weigh(i - 1, 3)
                    if step in (5, 9, 13) and 0 <= i < NT:
                        weigh(i, (step - 5) // 4)

        @block.tensor
        def _(pe):
            pe.wait_ge(cst_in, 16)
            pe.wait_ge(cst_bf, 5)
            for f in range(2):
                s = FS[f]
                logits = banks[:, 2, 0:NT * E].rearrange("p (i e) -> p i e", e=E)

                def x_turns(q):
                    pe.wait_ge(s["xn"], 2 * q + 2)
                    if q >= 2:
                        pe.wait_ge(s["xt_lo"], q - 1)
                    for c in range(2):
                        for k in range(KC):
                            at = (c * KC + k) * P
                            mm = pe.transpose(banks[:, q % 2, at:at + P], xn[:, 2 * q + c, k * P:k * P + P], ident)
                    mm.then_inc(s["xt_ps"], 1)

                def router(g):
                    pe.wait_ge(s["xt_lo"], 2 * g + 2)
                    if g == 0:
                        pe.wait_ge(split_res, 1)
                    if g >= 2:
                        pe.wait_ge(s["lt_sb"], g - 1)
                    o = banks[0:E, 6 + g % 2, :].rearrange("p (c t) -> p c t", c=4)
                    for k in range(KC):
                        w = slice(W_GATE + k * E, W_GATE + k * E + E)
                        mm = exact3(pe, o, wh[:, w], wl[:, w], xth[:, 4 * g:4 * g + 4, k, :],
                                    xtl[:, 4 * g:4 * g + 4, k, :], k == 0, k == KC - 1)
                    mm.then_inc(s["lt_ps"], 1)

                def logit_turns(g):
                    pe.wait_ge(s["lt_sb"], g + 1)
                    for c in range(4):
                        mm = pe.transpose(logits[:, 4 * g + c, :], turned_logits[:, g % 2, c * P:c * P + P],
                                          ident[0:E, 0:E])
                    mm.then_inc(s["logits"], 1)

                for q in range(4):
                    x_turns(q)
                router(0)
                for q in range(4, NT // 2):
                    x_turns(q)
                    if q % 2 == 1:
                        router(q // 2 - 1)
                        logit_turns(q // 2 - 2)
                router(3)
                logit_turns(2)
                logit_turns(3)

                def s_up(i):
                    if i == 0:
                        pe.wait_ge(split_res, 2)
                    else:
                        pe.wait_ge(s["shid"], i)
                    for k in range(KC):
                        for half in range(2):
                            at = W_SGU + (k * 2 + half) * SF
                            mm = exact3(pe, banks[:, 3 + half, 0:SF], xth[:, i, k, :], xtl[:, i, k, :],
                                        wh[:, at:at + SF], wl[:, at:at + SF], k == 0, k == KC - 1)
                    mm.then_inc(s["sgu"], 1)

                def s_turn(i):
                    pe.wait_ge(s["shid"], i + 1)
                    if i >= 1:
                        pe.wait_ge(s["sht_lo"], i)
                    for c in range(SC):
                        mm = pe.transpose(banks[:, 5, c * P:c * P + P], sh[:, c * P:c * P + P], ident)
                    mm.then_inc(s["sht_ps"], 1)

                def s_down(i):
                    pe.wait_ge(s["sht_lo"], i + 1)
                    if i == 0:
                        pe.wait_ge(split_res, 3)
                        pe.wait_ge(s["lt_sb"], 4)
                    if i >= 2:
                        pe.wait_ge(s["sx"], i - 1)
                    for c in range(SC):
                        at = W_SD + c * D
                        mm = exact3(pe, banks[:, 6 + i % 2, 0:D], shh[:, c * P:c * P + P], shl[:, c * P:c * P + P],
                                    wh[:, at:at + D], wl[:, at:at + D], c == 0, c == SC - 1)
                    mm.then_inc(s["sy"], 1)

                def find_ranks():
                    pe.wait_ge(s["picks"], 1)
                    ranks = banks[:, 2, 0:(NT + 1) * E].rearrange("p (i e) -> p i e", e=E)
                    pe.matmul(ranks, tri_bf[:], pick_bf[:], start=True, stop=False)
                    for i in range(NT):
                        mm = pe.matmul(ranks[:, i + 1:NT + 1, :], one_bf[:],
                                       pick_bf[:, i:i + 1, :].to_broadcast([P, NT - i, E]),
                                       start=False, stop=i == NT - 1)
                    mm.then_inc(s["ranks"], 1)

                s_up(0)
                s_turn(0)
                for i in range(1, NT):
                    s_up(i)
                    s_down(i - 1)
                    s_turn(i)
                    if i == 2:
                        find_ranks()
                s_down(NT - 1)

                eh2 = eh[:].rearrange("p e w -> p (e w)")
                el2 = el[:].rearrange("p e w -> p (e w)")

                def experts_of(p):
                    _, at = nc.values_load_multi_w_load_instructions(
                        tile_weights[0:1, 2 * p:2 * p + 4], engines=[mybir.EngineType.PE], min_val=0,
                        max_val=(E - 1) * EW, skip_runtime_bounds_check_because="the table holds expert offsets below the row length")
                    return at

                def turn(p):
                    n = p % 4
                    pe.wait_ge(s["xs_in"][n], (p // 4 + 1) * 16)
                    if p >= 1:
                        pe.wait_ge(s["ext_lo"], p)
                    for c in range(2):
                        for k in range(KC):
                            at = (c * KC + k) * P
                            mm = pe.transpose(banks[:, 0, at:at + P], xs[n][:, c, k * P:k * P + P], ident)
                    mm.then_inc(s["ext_ps"], 1)

                def up(p, par, which):
                    pe.wait_ge(s["ext_lo"], p + 1)
                    for c in range(2):
                        e = which[c]
                        for k in range(KC):
                            w, n = k * 2 * FF, 2 * FF
                            mm = exact3(pe, banks[:, 3 + c, 0:2 * FF], exh[par][:, c, k, :], exl[par][:, c, k, :],
                                        eh2[:, bass.ds(e + w, n)], el2[:, bass.ds(e + w, n)], k == 0, k == KC - 1)
                    mm.then_inc(s["egu"], 1)

                def h_turn(p):
                    pe.wait_ge(s["ehid"], p + 1)
                    for c in range(2):
                        for k in range(HC):
                            at = (c * HC + k) * P
                            mm = pe.transpose(banks[:, 5, at:at + P], ehid[:, c, k * P:k * P + P], ident)
                    mm.then_inc(s["eht_ps"], 1)

                def down(p, par, which):
                    pe.wait_ge(s["eht_lo"], p + 1)
                    for c in range(2):
                        e = which[c]
                        for k in range(HC):
                            w, n = EW_D + k * D, D
                            mm = exact3(pe, banks[:, 6 + par, c * D:(c + 1) * D], ehh[:, c, k, :], ehl[:, c, k, :],
                                        eh2[:, bass.ds(e + w, n)], el2[:, bass.ds(e + w, n)], k == 0, k == HC - 1)
                    mm.then_inc(s["ey"], 1)

                pe.wait_ge(s["slots"], 3)
                pe.wait_ge(split_exp, (f + 1) * E)
                turn(0)
                regs = {}
                for p in range(NP):
                    if p % 2 == 0:
                        four = experts_of(p)
                        regs[p], regs[p + 1] = four[0:2], four[2:4]
                    if p + 1 < NP:
                        turn(p + 1)
                    up(p, p % 2, regs[p])
                    if p >= 1:
                        down(p - 1, (p - 1) % 2, regs[p - 1])
                    h_turn(p)
                down(NP - 1, 1, regs[NP - 1])
                if f == 0:
                    attention_tensor(pe)

        def attention_vector(dve, link, norm_stats, norm_factors):
            s = AS
            norm_factors(s)
            dve.wait_ge(bias_in, 32)
            dve.wait_ge(s["mem"], 10)

            def clear(buffer):
                for h in (0, H // 2):
                    nc.vector.memset(buffer[:, h:h + H // 2, :].bitcast(F32), 0.0).then_inc(s["clear"], 1)

            def keep_q0(i):
                dve.wait_ge(s["q0_ps"], i + 1)
                if i < 2:
                    dve.wait_ge(s["clear"], 2 + 4 * i)
                nc.vector.tensor_copy(q0T[i % 2][64:112, 1:H:2, :], turned(64, 112)).then_inc(s["q0_odd"], 1)

            def keep_q(i):
                dve.wait_ge(s["qt_ps"], i + 1)
                if i < 2:
                    dve.wait_ge(s["clear"], 4 + 4 * i)
                nc.vector.tensor_copy(qT[i % 2][64:128, 1:H:2, :], turned(64, 128)).then_inc(s["qt_odd"], 1)

            def turned(a, b):
                return banks[a:b, 1:3, :].rearrange("p a (g t) -> p (a g) t", g=4)

            def normalise(i):
                if i >= 2:
                    dve.wait_ge(s["xt_ps"], i - 1)
                nc.vector.tensor_scalar(xa[i % 2][:], x[:, i, :], mv[:, i, 0:1], rstd[:, i:i + 1],
                                        ALU.subtract, ALU.mult).then_inc(s["xn"], 1)

            def x_lo(i):
                dve.wait_ge(s["xt_hi"], i + 1)
                nc.vector.tensor_tensor(xal[:], banks[:, 0, 0:D].rearrange("p (k t) -> p k t", k=KC),
                                        xah[:].bitcast(F32), ALU.subtract).then_inc(s["xt_lo"], 1)

            def add_bias(i):
                b, j = divmod(i, TB)
                dve.wait_ge(s["qkv"], i + 1)
                nc.vector.tensor_tensor(qk[:], banks[:, 1, :].rearrange("p (a h d) -> p a h d", a=2, h=H),
                                        bqkv[:, 0:2 * D].rearrange("p (a h d) -> p a h d", a=2, h=H), ALU.add)\
                    .then_inc(s["qk_sb"], 1)
                nc.vector.tensor_tensor(v[b % 2][:, j, :, 0:HD], banks[:, 2, 0:D].rearrange("p (h d) -> p h d", h=H),
                                        bqkv[:, 2 * D:3 * D].rearrange("p (h d) -> p h d", h=H), ALU.add)\
                    .then_inc(s["v_sb"], 1)

            def qk_lo(i):
                st = stack[i % 2]
                dve.wait_ge(s["hi"], i + 1)
                for part, at in ((1, 32), (0, 16)):
                    nc.vector.tensor_tensor(st[:, part, :, at:at + 16], qk[:, part, :, :],
                                            st[:, part, :, 0:16].bitcast(F32), ALU.subtract).then_inc(s["lo"], 1)

            def maximum(i, unit):
                n = (i % TB + 1) * P
                u = bound_base[i] + unit
                heads = bound_units(i)[unit]
                dve.wait_ge(s["s1"], u + 1)
                nc.vector.tensor_reduce(smax[:, heads[0]:heads[-1] + 1],
                                        banks[:, 3 + u % 2, 0:len(heads) * n].rearrange("p (h s) -> p h s", s=n),
                                        X, ALU.max).then_inc(s["mx"], 1)

            def put_maxima(i):
                st = stack[i % 2]
                dve.wait_ge(s["mx"], bound_base[i + 1])
                nc.vector.tensor_scalar(st[:, 0, :, 48], smax[:], -1.0, None, ALU.mult).then_inc(s["m_hi"], 1)
                dve.wait_ge(s["m_hi"], 2 * i + 1)
                nc.vector.scalar_tensor_tensor(st[:, 0, :, 49], smax[:], -1.0, st[:, 0, :, 48].bitcast(F32),
                                               ALU.mult, ALU.subtract).then_inc(s["m_hi"], 1)

            def divide(i):
                dve.wait_ge(s["o_ps"], i + 1)
                o = banks[:, 0, :].rearrange("p (h c) -> p h c", c=32)
                link(nc.vector.reciprocal(rden[:], o[:, :, 16]))
                nc.vector.tensor_tensor(ot[:], o[:, :, 0:HD], rden[:].unsqueeze(2).to_broadcast([P, H, HD]), ALU.mult)\
                    .then_inc(s["o_sb"], 1)

            def o_lo(i):
                dve.wait_ge(s["oc_hi"], i + 1)
                nc.vector.tensor_tensor(ol[:], banks[:, 0, 0:D].rearrange("p (k t) -> p k t", k=KC),
                                        oh[:].bitcast(F32), ALU.subtract).then_inc(s["oc_lo"], 1)

            def residual(i):
                dve.wait_ge(s["y"], i + 1)
                dve.wait_ge(s["bo"], i + 1)
                nc.vector.tensor_tensor(x[:, i, :], banks[:, 0, 0:D], x[:, i, :], ALU.add).then_inc(s["done"], 1)

            def row_stats(i):
                dve.wait_ge(s["done"], i + 1)
                norm_stats(i)

            normalise(0)
            after = {0: ((x_lo, 2),), 3: ((add_bias, 2),), 4: ((divide, -1),), 5: ((qk_lo, 2),), 7: ((o_lo, -1),),
                     9: ((residual, -1),), 10: ((put_maxima, 1), (row_stats, -1)), 11: ((keep_q0, 2),),
                     13: ((normalise, 3),), 14: ((keep_q, 1),)}
            for i in range(-2, NT + 1):
                for step in range(16):
                    if i == -2 and step in (1, 6, 10):
                        clear({1: qT[0], 6: q0T[1], 10: qT[1]}[step])
                    if 0 <= i + 1 < NT:
                        for unit in units_at(len(bound_units(i + 1)), step, 11):
                            maximum(i + 1, unit)
                    for part, ahead in after.get(step, ()):
                        if 0 <= i + ahead < NT:
                            part(i + ahead)
            dve.wait_ge(s["done"], NT)

        @block.vector
        def _(dve):
            def link(ins):
                links[0] += 1
                ins.then_inc(chain, 1)
                dve.wait_ge(chain, links[0])

            def norm_stats(i):
                nc.vector.bn_stats(stats[:, i, :], x[:, i, :]).then_inc(row_stats_in, 1)

            def norm_factors(s):
                norms[0] += NT
                dve.wait_ge(row_stats_in, norms[0])
                for i in range(NT):
                    ins = nc.vector.bn_aggr(mv[:, i, :], stats[:, i, :])
                link(ins)
                nc.vector.tensor_scalar(ve[:], mv[:, :, 1], EPS, None, ALU.add).then_inc(s["var"], 1)
                dve.wait_ge(s["sd"], 1)
                link(nc.vector.reciprocal(rstd[:], rstd[:]))
                link(nc.vector.tensor_tensor(nt1[:], ve[:], rstd[:], ALU.mult))
                link(nc.vector.tensor_tensor(nt2[:], nt1[:], rstd[:], ALU.mult))
                link(nc.vector.tensor_scalar(nt1[:], nt2[:], -0.5, 1.5, ALU.mult, ALU.add))
                link(nc.vector.tensor_tensor(rstd[:], rstd[:], nt1[:], ALU.mult))

            norms = [0]
            for i in range(NT):
                if i % TB == 0:
                    dve.wait_ge(x_in_s[i // TB], 16)
                norm_stats(i)
            dve.wait_ge(cst_in, 16)
            for dst, at in ((tri_bf, C_U), (one_bf, C_ONE), (id_bf, C_ID), (mask_bf, C_MASK), (id_r, C_ID)):
                nc.vector.tensor_copy(dst[:], cst[:, at:at + P]).then_inc(cst_bf, 1)

            for f in range(2):
                s = FS[f]
                r = route
                norm_factors(s)
                for q in range(NT // 2 + 1):
                    if q < NT // 2:
                        for i in (2 * q, 2 * q + 1):
                            nc.vector.tensor_scalar(xn[:, i, :], x[:, i, :], mv[:, i, 0:1], rstd[:, i:i + 1],
                                                    ALU.subtract, ALU.mult).then_inc(s["xn"], 1)
                    if q >= 1:
                        p = q - 1
                        dve.wait_ge(s["xt_hi"], p + 1)
                        nc.vector.tensor_tensor(xtl[:, 2 * p:2 * p + 2, :, :],
                                                banks[:, p % 2, :].rearrange("p (c k t) -> p c k t", c=2, k=KC),
                                                xth[:, 2 * p:2 * p + 2, :, :].bitcast(F32), ALU.subtract)\
                            .then_inc(s["xt_lo"], 1)
                iota = cst[:, C_IOTA:C_IOTA + NT * E].rearrange("p (i e) -> p i e", e=E)

                def wide(ap):
                    return ap[:].unsqueeze(2).to_broadcast([P, NT, E])

                def pick(m, hot):
                    nc.vector.tensor_reduce(r[m][:], r["lg"][:], X, ALU.max).then_inc(s["sig_in"], 1)
                    dve.wait_ge(s["sig_in"], 1 if m == "m1" else 2)
                    link(nc.vector.tensor_tensor(r["c"][:], r["lg"][:], wide(r[m]), ALU.is_equal))
                    link(nc.vector.scalar_tensor_tensor(r["c"][:], r["c"][:], -float(E), iota, ALU.mult, ALU.add))
                    link(nc.vector.tensor_reduce(r["i1"][:], r["c"][:], X, ALU.min))
                    link(nc.vector.tensor_scalar(r["i1"][:], r["i1"][:], float(E), None, ALU.add))
                    link(nc.vector.tensor_tensor(r[hot][:], iota, wide(r["i1"]), ALU.is_equal))

                def first_pick():
                    link(nc.vector.tensor_copy(r["lg"][:], banks[:, 2, 0:NT * E].rearrange("p (i e) -> p i e", e=E)))
                    pick("m1", "oh1")

                def second_pick():
                    link(nc.vector.scalar_tensor_tensor(r["lg"][:], r["oh1"][:], -BIG, r["lg"][:], ALU.mult, ALU.add))
                    pick("m2", "oh2")
                    nc.vector.tensor_tensor(pick_bf[:, 0:NT, :], r["oh1"][:], r["oh2"][:], ALU.add)\
                        .then_inc(s["picks"], 1)

                def pick_weights():
                    dve.wait_ge(s["sig"], 2)
                    link(nc.vector.scalar_tensor_tensor(r["den"][:], r["w1"][:], 1e-20, r["w2"][:], ALU.add, ALU.add))
                    link(nc.vector.reciprocal(r["den"][:], r["den"][:]))
                    for w in ("w1", "w2"):
                        link(nc.vector.scalar_tensor_tensor(r[w][:], r[w][:], 1.25, r["den"][:], ALU.mult, ALU.mult))

                def expert_tiles():
                    dve.wait_ge(s["ranks"], 1)
                    link(nc.vector.tensor_copy(r["rk"][:], banks[:, 2, 0:(NT + 1) * E].rearrange("p (i e) -> p i e", e=E)))
                    link(nc.vector.tensor_tensor(r["cnt"][:], r["rk"][:, NT, :].unsqueeze(2).to_broadcast([P, E, NT]),
                                                 cst[:, C_THR:C_THR + E * NT].rearrange("p (e j) -> p e j", e=E), ALU.is_gt))
                    link(nc.vector.tensor_reduce(r["te"][:], r["cnt"][:], X, ALU.add))
                    link(nc.vector.tensor_tensor(r["ee"][:], cst[:, C_TRI:C_TRI + E * E].rearrange("p (a b) -> p a b", a=E),
                                                 r["te"][:].unsqueeze(1).to_broadcast([P, E, E]), ALU.mult))
                    link(nc.vector.tensor_reduce(r["inc"][:], r["ee"][:], X, ALU.add))
                    link(nc.vector.tensor_tensor(r["te"][:], r["inc"][:], r["te"][:], ALU.subtract))
                    link(nc.vector.scalar_tensor_tensor(r["rk"][:, 0:NT, :], r["te"][:].unsqueeze(1).to_broadcast([P, NT, E]),
                                                        float(P), r["rk"][:, 0:NT, :], ALU.mult, ALU.add))

                def pick_slots():
                    for hot, sl, slot in (("oh1", "sl1", slot1), ("oh2", "sl2", slot2)):
                        link(nc.vector.tensor_tensor(r["c"][:], r[hot][:], r["rk"][:, 0:NT, :], ALU.mult))
                        link(nc.vector.tensor_reduce(r[sl][:], r["c"][:], X, ALU.add))
                        nc.vector.tensor_copy(slot[:], r[sl][:]).then_inc(s["slots"], 1)

                def tile_offsets():
                    link(nc.vector.tensor_tensor(r["tb"][:], r["inc"][0:1, :].unsqueeze(1).to_broadcast([1, 2 * NP, E]),
                                                 cst[0:1, C_J:C_J + 2 * NP * E].rearrange("p (j e) -> p j e", e=E),
                                                 ALU.is_le))
                    link(nc.vector.tensor_reduce(r["tf"][:], r["tb"][:], X, ALU.add))
                    link(nc.vector.tensor_scalar(r["tf"][:], r["tf"][:], float(E - 1), float(EW), ALU.min, ALU.mult))
                    nc.vector.tensor_copy(tile_weights[:], r["tf"][:]).then_inc(s["slots"], 1)
                def s_out(i):
                    dve.wait_ge(s["sy"], i + 1)
                    nc.vector.scalar_tensor_tensor(x[:, i, :], banks[:, 6 + i % 2, 0:D], 0.5, x[:, i, :],
                                                   ALU.mult, ALU.add).then_inc(s["sx"], 1)

                dve.wait_ge(s["logits"], 4)
                nc.vector.memset(sh[:, SF:SC * P], 0.0)
                nc.vector.memset(pick_bf[:, NT, :], 0.0)
                routing = {0: first_pick, 1: second_pick, 2: pick_weights, 3: expert_tiles, 4: pick_slots,
                           5: tile_offsets}
                for i in range(NT):
                    dve.wait_ge(s["ssilu"], i + 1)
                    if i >= 1:
                        dve.wait_ge(s["sht_ps"], i)
                    nc.vector.tensor_tensor(sh[:, 0:SF], sg[:], banks[:, 4, 0:SF], ALU.mult).then_inc(s["shid"], 1)
                    if i >= 1:
                        s_out(i - 1)
                    dve.wait_ge(s["sht_hi"], i + 1)
                    nc.vector.tensor_tensor(shl[:], banks[:, 5, 0:SC * P], shh[:].bitcast(F32), ALU.subtract)\
                        .then_inc(s["sht_lo"], 1)
                    if i in routing:
                        routing[i]()
                    if 5 <= i < 5 + E:
                        n = N_RES + f * E + i - 5
                        dve.wait_ge(split_hi, n + 1)
                        piece_lo(nc.vector, n)
                s_out(NT - 1)

                link(nc.vector.memset(ehid[:], 0.0))

                def x_lo(p, par):
                    dve.wait_ge(s["ext_hi"], p + 1)
                    nc.vector.tensor_tensor(exl[par][:], banks[:, 0, :].rearrange("p (c k t) -> p c k t", c=2, k=KC),
                                            exh[par][:].bitcast(F32), ALU.subtract).then_inc(s["ext_lo"], 1)

                def hidden(p):
                    dve.wait_ge(s["esilu"], p + 1)
                    nc.vector.tensor_tensor(ehid[:, :, 0:FF], eg[:], banks[:, 3:5, FF:2 * FF], ALU.mult)\
                        .then_inc(s["ehid"], 1)

                def h_lo(p):
                    dve.wait_ge(s["eht_hi"], p + 1)
                    nc.vector.tensor_tensor(ehl[:], banks[:, 5, :].rearrange("p (c k t) -> p c k t", c=2, k=HC),
                                            ehh[:].bitcast(F32), ALU.subtract).then_inc(s["eht_lo"], 1)

                def y_out(p, par, stores):
                    dve.wait_ge(s["ey"], p + 1)
                    if stores is not None:
                        dve.wait_ge(s["y_out"][par], stores * 16)
                    nc.vector.tensor_copy(ys[par][:], banks[:, 6 + par, :].rearrange("p (c d) -> p c d", c=2))\
                        .then_inc(s["ey_sb"], 1)

                x_lo(0, 0)
                x_lo(1, 1)
                hidden(0)
                h_lo(0)
                x_lo(2, 0)
                hidden(1)
                y_out(0, 0, None)
                h_lo(1)
                x_lo(3, 1)
                hidden(2)
                y_out(1, 1, None)
                h_lo(2)
                with dve.Fori(0, NP // 2 - 2) as m:
                    i = 2 * m + 3
                    for d, par in ((0, 1), (1, 0)):
                        x_lo(i + d + 1, 1 - par)
                        hidden(i + d)
                        y_out(i + d - 1, 1 - par, m + 1)
                        h_lo(i + d)
                hidden(NP - 1)
                y_out(NP - 2, 0, NP // 2 - 1)
                h_lo(NP - 1)
                y_out(NP - 1, 1, NP // 2 - 1)
                for i in range(NT):
                    dve.wait_ge(s["pick_in"][i % 4], 32 * (i // 4 + 1))
                    link(nc.vector.scalar_tensor_tensor(x[:, i, :], picked[i % 4][0][:], r["w1"][:, i:i + 1],
                                                        x[:, i, :], ALU.mult, ALU.add))
                    nc.vector.scalar_tensor_tensor(x[:, i, :], picked[i % 4][1][:], r["w2"][:, i:i + 1],
                                                   x[:, i, :], ALU.mult, ALU.add).then_inc(s["combined"], 1)
                    if f == 0 and i >= 1:
                        dve.wait_ge(s["combined"], i)
                        norm_stats(i - 1)
                if f == 0:
                    dve.wait_ge(s["combined"], NT)
                    norm_stats(NT - 1)
                    attention_vector(dve, link, norm_stats, norm_factors)


def constants():
    c = np.zeros((P, C_END), np.float32)
    r = np.arange(P)
    c[:, C_ID:C_ID + P] = np.eye(P)
    c[:, C_U:C_U + P] = r[:, None] < r[None, :]
    c[:, C_ONE:C_ONE + P] = 1.0
    c[:, C_MASK:C_MASK + P] = np.where(r[None, :] > r[:, None], -BIG, 0.0)
    c[:, C_IOTA:C_IOTA + NT * E] = np.tile(np.arange(E), NT)
    c[:, C_THR:C_THR + E * NT] = np.tile(P * np.arange(NT), E)
    c[:, C_TRI:C_TRI + E * E] = (np.arange(E)[None, :] <= np.arange(E)[:, None]).reshape(-1)
    c[:, C_J:C_J + 2 * NP * E] = np.repeat(np.arange(2 * NP), E)
    return c


def rows_by_chunk(w):
    k = w.shape[0] // P
    return w.reshape(k, P, -1).transpose(1, 0, 2).reshape(P, -1)


def padded(w, rows):
    return np.concatenate([w, np.zeros((rows - w.shape[0], w.shape[1]), w.dtype)])


def kernel(**inputs):
    import concourse.bacc as bacc
    from concourse.bass_utils import run_bass_kernel_spmd as run

    a = {k.replace("L0_", ""): np.asarray(v) for k, v in inputs.items()}
    resident = np.concatenate([
        rows_by_chunk(a["ffn_gate_w"].T),
        rows_by_chunk(np.concatenate([a["ffn_shared_wg"], a["ffn_shared_wu"]]).T),
        rows_by_chunk(padded(a["ffn_shared_wd"].T, SC * P)),
        rows_by_chunk(a["attn_Wqkv"]),
        rows_by_chunk(a["attn_Wo"])], axis=1)
    experts = np.stack([np.concatenate([
        rows_by_chunk(np.concatenate([a["ffn_exp_wg"][e], a["ffn_exp_wu"][e]]).T),
        rows_by_chunk(padded(a["ffn_exp_wd"][e].T, HC * P))], axis=1) for e in range(E)], axis=1)
    arrays = {
        "x_in": a["attn_x"], "w_res": resident, "w_exp": experts,
        "bias_qkv": np.broadcast_to(a["attn_bqkv"], (P, 3 * D)), "bias_o": np.broadcast_to(a["attn_bo"], (P, D)),
        "consts": constants()}
    arrays = {k: np.ascontiguousarray(v) for k, v in arrays.items()}
    nc = bacc.Bacc("TRN2", target_bir_lowering=False, num_devices=1)
    aps = [nc.dram_tensor(k, v.shape, F32, kind="ExternalInput").ap() for k, v in arrays.items()]
    out = nc.dram_tensor("out", (B, S, D), F32, kind="ExternalOutput").ap()
    build(nc, *aps, out)
    return run(nc, [arrays], core_ids=[0]).results[0]["out"]
```

```python
from contextlib import ExitStack

import numpy as np
import concourse.bass as bass
from concourse import mybir

F32 = mybir.dt.float32
F32R = mybir.dt.float32r
BF16 = mybir.dt.bfloat16
U32 = mybir.dt.uint32
I32 = mybir.dt.int32
ALU = mybir.AluOpType
ACT = mybir.ActivationFunctionType
X = mybir.AxisListType.X

P = 128
B, S, D = 4, 512, 256
T = B * S
NT = T // P
TB = S // P
KC = D // P
H, HD = 16, 16
E, FF, SF = 8, 176, 352
HC = 2
SC = 3
EPS = 1e-5
BIG = 1e30
POOL_PIECES = (0, 2)
MAX_TILES = (2 * T + E * (P - 1)) // P
NP = (MAX_TILES + 1) // 2
LOAD_ROUNDS = NP // 4 - 1
BLANK_TILES = 2 * NP // LOAD_ROUNDS
assert BLANK_TILES * LOAD_ROUNDS == 2 * NP
ROWS = NP * 2 * P
RW = D + 2

W_GATE = 0
W_SGU = W_GATE + KC * E
W_SD = W_SGU + KC * 2 * SF
W_QKV = W_SD + SC * D
W_O = W_QKV + KC * 3 * D
W_END = W_O + KC * D
EW_D = KC * 2 * FF
EW = EW_D + HC * D
STAGE = 1536

C_ID, C_U, C_ONE, C_MASK, C_IOTA = 0, P, 2 * P, 3 * P, 4 * P
C_THR = C_IOTA + NT * E
C_TRI = C_THR + E * NT
C_J = C_TRI + E * E
C_TOKEN = C_J + 2 * NP * E
C_TILE = C_TOKEN + NT
C_END = C_TILE + 2 * NP


def resident_chunks():
    return [(W_GATE, W_SGU), (W_SGU, W_SD), (W_SD, W_QKV), (W_QKV, W_O), (W_O, W_END)]


def bound_units(i):
    per = TB // (i % TB + 1)
    return [list(range(h, h + per)) for h in range(0, H, per)]


def score_units(i):
    blocks = [(pair, t) for pair in range(H // 2) for t in range(i % TB + 1)]
    return [blocks[n:n + 2] for n in range(0, len(blocks), 2)]


def units_at(n, step, steps):
    return [u for u in range(n) if u * steps // n == step]


def build(nc, x_in, w_res, w_exp, bias_qkv, bias_o, consts, out):
    sorted_x = [nc.dram_tensor(f"sorted_x{f}", (ROWS, RW), F32, kind="Internal").ap() for f in range(2)]
    token_y = nc.dram_tensor("token_y", (2 * T + ROWS, D), F32, kind="Internal").ap()

    with ExitStack() as ctx:
        def sem(name):
            return ctx.enter_context(nc.semaphore(name))

        def sb(name, shape, dt, where=ctx):
            return where.enter_context(nc.sbuf_tensor(name, shape, dt))

        x = sb("x", [P, NT, D], F32)
        wh = sb("wh", [P, W_END], F32R)
        wl = sb("wl", [P, W_END], F32R)
        cst = sb("cst", [P, C_END], F32)
        tri_bf = sb("tri_bf", [P, P], BF16)
        one_bf = sb("one_bf", [P, P], BF16)
        id_r = sb("id_r", [P, P], F32R)
        id_bf = sb("id_bf", [P, P], BF16)
        mask_bf = sb("mask_bf", [P, P], BF16)
        stats = sb("stats", [P, NT, 6], F32)
        mv = sb("mv", [P, NT, 2], F32)
        ve = sb("ve", [P, NT], F32)
        rstd = sb("rstd", [P, NT], F32)
        shift = sb("shift", [P, NT], F32)
        nt1 = sb("nt1", [P, NT], F32)
        nt2 = sb("nt2", [P, NT], F32)
        w1 = sb("w1", [P, NT], F32)
        w2 = sb("w2", [P, NT], F32)
        ident = cst[:, C_ID:C_ID + P]
        banks = ctx.enter_context(nc.psum_tensor("banks", [P, 8, 512], F32))

        ffn_ctx = ExitStack()
        eh = sb("eh", [P, E, EW], F32R, ffn_ctx)
        el = sb("el", [P, E, EW], F32R, ffn_ctx)
        stage = [sb(f"stage{n}", [P, STAGE], F32, ffn_ctx) for n in range(2)]
        xn = sb("xn", [P, NT, RW], F32, ffn_ctx)
        blank = sb("blank", [P, RW], F32, ffn_ctx)
        route = {}
        for name, shape, dt in (
                ("lg", [P, NT, E], F32), ("c", [P, NT, E], F32), ("oh1", [P, NT, E], F32), ("oh2", [P, NT, E], F32),
                ("m1", [P, NT], F32), ("m2", [P, NT], F32), ("i1", [P, NT], F32),
                ("den", [P, NT], F32),
                ("cnt", [P, E, NT], F32), ("te", [P, E], F32), ("ee", [P, E, E], F32), ("inc", [P, E], F32),
                ("rk", [P, NT + 1, E], F32), ("sl1", [P, NT], F32), ("sl2", [P, NT], F32),
                ("tb", [P, 2 * NP, E], F32), ("tf", [P, 2 * NP], F32), ("to", [1, 2 * NP], F32),
                ("goal", [P, 2 * NP], F32), ("same", [P, 2 * NP], F32), ("fill", [P, 2 * NP], F32)):
            route[name] = sb("r_" + name, shape, dt, ffn_ctx)
        pick_bf = sb("pick_bf", [P, NT + 1, E], BF16, ffn_ctx)
        slot1 = sb("slot1", [P, NT], U32, ffn_ctx)
        slot2 = sb("slot2", [P, NT], U32, ffn_ctx)
        marks = sb("marks", [P, 2 * NP, 2], F32, ffn_ctx)
        goal = sb("goal", [P, 2 * NP], U32, ffn_ctx)
        tile_weights = sb("tile_weights", [1, 2 * NP], I32, ffn_ctx)
        s_ctx = ExitStack()
        xth = sb("xth", [P, NT, KC, P], F32R, s_ctx)
        xtl = sb("xtl", [P, NT, KC, P], F32R, s_ctx)
        l_ctx = ExitStack()
        turned_logits = sb("turned_logits", [E, 2, 4 * P], F32, l_ctx)
        l_ctx.close()
        sg = sb("sg", [P, SF], F32, s_ctx)
        sh = sb("sh", [P, SC * P], F32, s_ctx)
        shh = sb("shh", [P, SC * P], F32R, s_ctx)
        shl = sb("shl", [P, SC * P], F32R, s_ctx)
        s_ctx.close()
        e_ctx = ExitStack()
        exh = [sb(f"exh{n}", [P, 2, KC, P], F32R, e_ctx) for n in range(2)]
        exl = [sb(f"exl{n}", [P, 2, KC, P], F32R, e_ctx) for n in range(2)]
        eg = sb("eg", [P, 2, FF], F32, e_ctx)
        ehid = sb("ehid", [P, 2, HC * P], F32, e_ctx)
        ehh = sb("ehh", [P, 2, HC, P], F32R, e_ctx)
        ehl = sb("ehl", [P, 2, HC, P], F32R, e_ctx)
        ys = [sb(f"ys{n}", [P, 2, D], F32, e_ctx) for n in range(2)]
        e_ctx.close()
        xs = [stage[n // 2][:, n % 2 * 2 * D:(n % 2 + 1) * 2 * D].rearrange("p (c d) -> p c d", c=2) for n in range(4)]
        ffn_ctx.close()

        a_ctx = ExitStack()
        bqkv = sb("bqkv", [P, 3 * D], F32, a_ctx)
        bo = sb("bo", [P, D], F32, a_ctx)
        xa = [sb(f"xa{n}", [P, D], F32, a_ctx) for n in range(2)]
        xah = sb("xah", [P, KC, P], F32R, a_ctx)
        xal = sb("xal", [P, KC, P], F32R, a_ctx)
        qk = sb("qk", [P, 2, H, HD], F32, a_ctx)
        stack = [sb(f"stack{n}", [P, 2, H, 64], F32R, a_ctx) for n in range(3)]
        kT = [sb(f"kT{n}", [P, H // 2, S], F32R, a_ctx) for n in range(2)]
        qT = [sb(f"qT{n}", [P, H, P], F32R, a_ctx) for n in range(4)]
        mask_row = sb("mask_row", [P, S], F32, a_ctx)
        masked = [sb(f"masked{n}", [P, S], BF16, a_ctx) for n in range(2)]
        m_neg = sb("m_neg", [P, 2, 2, H // 2], F32R, a_ctx)
        mT = [sb(f"mT{n}", [2 * H, P], F32R, a_ctx) for n in range(2)]
        v = [sb(f"v{n}", [P, TB, H, 32], F32, a_ctx) for n in range(2)]
        smax = [sb(f"smax{n}", [P, H], F32, a_ctx) for n in range(2)]
        NPR = 8
        prob_all = sb("prob", [P, NPR, 512], F32, a_ctx)
        prob = [prob_all[:, n, :] for n in range(NPR)]
        oT = sb("oT", [P, TB, P], F32, a_ctx)
        rden = sb("rden", [P, H], F32, a_ctx)
        ot = sb("ot", [P, H, HD], F32, a_ctx)
        oh = sb("oh", [P, KC, P], F32R, a_ctx)
        ol = sb("ol", [P, KC, P], F32R, a_ctx)
        a_ctx.close()
        picked = [[prob_all[:, 4 * n + 2 * k:4 * n + 2 * k + 2, :].rearrange("p a b -> p (a b)")
                   .rearrange("p (c d) -> p c d", d=D) for k in range(2)] for n in range(2)]

        spare = eh[:].rearrange("p e w -> p (e w)").bitcast(F32)

        def picks_of(g, f):
            if f == 0 or g < 2:
                return picked[g % 2]
            return [spare[:, (2 * (g % 2) + k) * 4 * D:(2 * (g % 2) + k + 1) * 4 * D].rearrange("p (c d) -> p c d", d=D)
                    for k in range(2)]

        cst_in, bias_in, blank_set = (sem(n) for n in ("cst_in", "bias_in", "blank_set"))
        blanked = [sem("blanked0"), sem("blanked1")]
        x_in_s = [sem(f"x_in_s{b}") for b in range(B)]
        stored = sem("stored")
        cst_bf = sem("cst_bf")
        chain = sem("chain")
        row_stats_in = sem("row_stats_in")
        staged = [sem("staged0"), sem("staged1")]
        split_hi = sem("split_hi")
        split_res = sem("split_res")
        split_exp = sem("split_exp")

        FS = []
        for f in range(2):
            FS.append({n: sem(f"{n}_{f}") for n in (
                "var", "sd", "xn", "xn_odd", "xt_ps", "xt_hi", "xt_lo", "lt_ps", "lt_sb", "logits", "picks", "ranks", "slots",
                "sig_in", "sig", "sgate", "sup", "ssilu", "shid", "sht_ps", "sht_hi", "sht_lo", "sy", "sx",
                "scattered", "marks_in", "goals", "ext_ps", "ext_hi", "ext_lo", "egu", "esilu", "ehid", "eht_ps", "eht_hi",
                "eht_lo", "ey", "ey_sb", "combined")})
            for name, count in (("y_out", 2), ("pick_in", 2), ("xs_in", 4)):
                FS[f][name] = [sem(f"{name}{n}_{f}") for n in range(4 if name == "pick_in" and f == 1 else count)]
        AS = {n: sem("a_" + n) for n in (
            "var", "sd", "xn", "xt_ps", "xt_hi", "xt_lo", "qkv", "qk_sb", "v_sb", "hi", "lo", "dup",
            "kt_ps", "kt_sb", "qt_ps", "q_even", "q_odd", "s1", "mx", "mt_ps", "mt_sb", "causal",
            "clear", "rstd", "s2", "p", "av", "ot_ps_in",
            "o_ps", "o_sb", "oc_ps", "oc_hi", "oc_lo", "y", "done", "mem", "bo", "m_hi")}

        AS["m_in"] = [sem(f"a_m_in{n}") for n in range(2)]
        block = ctx.enter_context(nc.Block())
        links = [0]
        bound_base = [sum(len(bound_units(t)) for t in range(i)) for i in range(NT + 1)]
        score_base = [sum(len(score_units(t)) for t in range(i)) for i in range(NT + 1)]

        pieces = []
        for a, b in resident_chunks():
            pieces.append((w_res[:, a:b], wh[:, a:b], wl[:, a:b]))
        N_RES = len(pieces)
        for f in range(2):
            for e in range(E):
                pieces.append((w_exp[:, e, :], eh[:, e, :], el[:, e, :]))

        expert_split = ((7, 8, 9, 10, 11, 12, 13, 14), (1, 3, 7, 8, 10, 11, 13, 14))

        def piece_dma(eng, n):
            src, hi, _ = pieces[n]
            if n >= 2:
                if n - 2 < N_RES:
                    eng.wait_ge(split_res, n - 1)
                else:
                    eng.wait_ge(split_exp, 2 * (n - 1 - N_RES))
            eng.dma_start(stage[n % 2][:, 0:hi.shape[1]], src).then_inc(staged[n % 2], 16)

        def piece_hi(n):
            _, hi, _ = pieces[n]
            nc.scalar.wait_ge(staged[n % 2], 16 * (n // 2 + 1))
            nc.scalar.activation(hi, stage[n % 2][:, 0:hi.shape[1]], ACT.Copy).then_inc(split_hi, 1)

        def piece_lo(eng, n, part, parts):
            _, hi, lo = pieces[n]
            w = hi.shape[1] // parts
            at = slice(part * w, part * w + w)
            eng.tensor_tensor(lo[:, at], stage[n % 2][:, at], hi[:, at].bitcast(F32), ALU.subtract)\
                .then_inc(split_res if n < N_RES else split_exp, 1)

        def exact3(pe, out_ap, xhi, xlo, whi, wlo, first, last):
            pe.matmul(out_ap, xhi, whi, start=first, stop=False)
            pe.matmul(out_ap, xhi, wlo, start=False, stop=False)
            return pe.matmul(out_ap, xlo, whi, start=False, stop=last)

        def attention_sync(sp):
            s = AS
            with sp.Fori(0, NT // 4) as m:
                for n in range(4):
                    sp.wait_ge(s["mt_sb"], 4 * m + n + 1)
                    for odd in range(2):
                        for low in range(2):
                            row, at = 64 * odd + 48 + low, (2 * odd + low) * (H // 2)
                            sp.dma_start(qT[n][row:row + 1, odd:H:2, :].bitcast(F32),
                                         mT[n % 2][at:at + H // 2, :].bitcast(F32))\
                                .then_inc(s["m_in"][n % 2], 16)

        @block.sync
        def _(sp):
            for b in range(B):
                sp.dma_start(x[:, TB * b:TB * b + TB, :],
                             x_in[b].rearrange("(i p) d -> p i d", p=P)).then_inc(x_in_s[b], 16)
            sp.dma_start(cst[:], consts).then_inc(cst_in, 16)
            for n in range(N_RES):
                piece_dma(sp, n)
            sp.wait_ge(blank_set, 3)

            def write_blanks(f, first, tiles):
                sp.dma_start(sorted_x[f][bass.ds(first * P, tiles * P), :].rearrange("(r q) d -> q r d", q=P),
                             blank[:].unsqueeze(1).to_broadcast([P, tiles, RW])).then_inc(blanked[f], 16)

            write_blanks(0, 0, 2 * NP)
            for f in range(2):
                s = FS[f]
                if f == 1:
                    sp.wait_ge(AS["done"], NT)
                for e in range(E):
                    piece_dma(sp, N_RES + f * E + e)
                sp.wait_ge(s["scattered"], 32 * NT)
                def load(p, n):
                    sp.dma_start(xs[n], sorted_x[f][bass.ds(p * (2 * P), 2 * P), 0:D]
                                 .rearrange("(c q) d -> q c d", q=P)).then_inc(s["xs_in"][n], 16)

                sp.wait_ge(split_exp, 2 * E * (f + 1))
                load(0, 0)
                load(1, 1)
                sp.dma_start(marks[:], sorted_x[f][:, D:RW].rearrange("(r q) d -> q r d", q=P))\
                    .then_inc(s["marks_in"], 16)
                load(2, 2)
                load(3, 3)
                with sp.Fori(0, LOAD_ROUNDS) as m:
                    i = 4 * m
                    for n in range(4):
                        sp.wait_ge(s["ext_ps"], i + n + 1)
                        load(i + n + 4, n)
                    if f == 0:
                        write_blanks(1, m * BLANK_TILES, BLANK_TILES)
                def load_picks(g):
                    for k in range(2):
                        sp.dma_start(picks_of(g, f)[k],
                                     token_y[k * T + g * S:k * T + (g + 1) * S, :].rearrange("(i p) d -> p i d", p=P))\
                            .then_inc(s["pick_in"][g % len(s["pick_in"])], 16)

                for par in range(2):
                    sp.wait_ge(s["y_out"][par], 16 * NP)
                for g in range(2 if f == 0 else B):
                    load_picks(g)
                if f == 0:
                    sp.dma_start(bqkv[:], bias_qkv).then_inc(bias_in, 16)
                    sp.dma_start(bo[:], bias_o).then_inc(bias_in, 16)
                if f == 0:
                    for g in range(2):
                        sp.wait_ge(s["combined"], 4 * g + 4)
                        load_picks(g + 2)
                    attention_sync(sp)
                else:
                    stores = [(g, 0, TB) for g in range(B - 1)] + [(B - 1, 0, TB // 2), (B - 1, TB // 2, TB)]
                    for g, a, b in stores:
                        sp.wait_ge(s["combined"], TB * g + b)
                        sp.dma_start(out[g, a * P:b * P, :].rearrange("(i p) d -> p i d", p=P),
                                     x[:, TB * g + a:TB * g + b, :]).then_inc(stored, 16)
                    sp.wait_ge(stored, 16 * len(stores))

        def attention_pool(pool):
            s = AS
            def clear(n):
                for h in (0, H // 2):
                    nc.gpsimd.memset(qT[n][:, h:h + H // 2, :].bitcast(F32), 0.0).then_inc(s["clear"], 1)

            def qk_lo(i):
                st = stack[i % 3]
                pool.wait_ge(s["hi"], i + 1)
                for part, at in ((1, 32), (0, 16)):
                    nc.gpsimd.tensor_tensor(st[:, part, :, at:at + 16], qk[:, part, :, :],
                                            st[:, part, :, 0:16].bitcast(F32), ALU.subtract).then_inc(s["lo"], 1)

            def add_bo(i):
                pool.wait_ge(s["xn"], i + 1)
                nc.gpsimd.tensor_tensor(x[:, i, :], x[:, i, :], bo[:], ALU.add).then_inc(s["bo"], 1)

            def causal(i, unit):
                u = score_base[i] + unit
                for a, (pair, t) in enumerate(score_units(i)[unit]):
                    if t == i % TB:
                        pool.wait_ge(s["p"], u + 1)
                        w = prob[u % NPR][:, a * 2 * P:(a + 1) * 2 * P].rearrange("p (h q) -> p h q", h=2)
                        nc.gpsimd.affine_select(out=w, in_=w, pattern=[[0, 2], [1, P]], compare_op=ALU.is_ge,
                                                fill=0.0, base=0, channel_multiplier=-1).then_inc(s["causal"], 1)

            def normalise(i):
                pool.wait_ge(s["rstd"], 1 if i < 1 else 2 if i < TB else 3)
                if i >= 2:
                    pool.wait_ge(s["xt_ps"], i - 1)
                nc.gpsimd.tensor_scalar(xa[i % 2][:], x[:, i, :], mv[:, i, 0:1], rstd[:, i:i + 1],
                                        ALU.subtract, ALU.mult).then_inc(s["xn"], 1)

            for par in range(2):
                pool.wait_ge(FS[0]["y_out"][par], 16 * NP)
            pool.wait_ge(blanked[1], 16 * LOAD_ROUNDS)
            for n in range(3):
                nc.gpsimd.memset(stack[n][:, 0, :, 48:64].bitcast(F32), 0.0).then_inc(s["mem"], 1)
                nc.gpsimd.memset(stack[n][:, 1, :, 48:50].bitcast(F32), 1.0).then_inc(s["mem"], 1)
                nc.gpsimd.memset(stack[n][:, 1, :, 50:64].bitcast(F32), 0.0).then_inc(s["mem"], 1)
            for n in range(2):
                nc.gpsimd.memset(v[n][:, :, :, 16:17], 1.0).then_inc(s["mem"], 1)
                nc.gpsimd.memset(v[n][:, :, :, 17:32], 0.0).then_inc(s["mem"], 1)
            clear(0)
            normalise(0)
            pool.wait_ge(bias_in, 32)
            add_bo(0)
            clear(1)

            after = {12: ((normalise, 5), (add_bo, 5)), 15: ((qk_lo, 4),)}
            for i in range(-4, NT + 1):
                for step in range(16):
                    if 0 <= i < NT:
                        for unit in units_at(len(score_units(i)), step, 16):
                            causal(i, unit)
                    if (i, step) in ((-4, 15), (-3, 2)):
                        clear(2 if i == -4 else 3)
                    for part, ahead in after.get(step, ()):
                        if 0 <= i + ahead < NT:
                            part(i + ahead)

        @block.gpsimd
        def _(pool):
            nc.gpsimd.memset(blank[:, 0:D], 0.0).then_inc(blank_set, 1)
            nc.gpsimd.memset(blank[:, D + 1:RW], -1.0).then_inc(blank_set, 1)
            pool.wait_ge(cst_in, 16)
            nc.gpsimd.tensor_scalar(blank[:, D:D + 1], cst[:, C_TOKEN:C_TOKEN + 1], float(T), None, ALU.add)\
                .then_inc(blank_set, 1)
            for n in range(N_RES):
                pool.wait_ge(split_hi, n + 1)
                piece_lo(nc.gpsimd, n, 0, 1)
            for f in range(2):
                s = FS[f]
                for n in range(N_RES + f * E, N_RES + f * E + POOL_PIECES[f]):
                    pool.wait_ge(split_hi, n + 1)
                    for part in range(2):
                        piece_lo(nc.gpsimd, n, part, 2)
                pool.wait_ge(blanked[f], 16 * LOAD_ROUNDS if f else 16)
                pool.wait_ge(s["xn_odd"], NT // 2)
                for n, slot in enumerate((slot1, slot2)):
                    pool.wait_ge(s["slots"], n + 1)
                    for i in range(NT):
                        pool.indirect_dma_start(
                            out=sorted_x[f], out_offset=bass.IndirectOffsetOnAxis(ap=slot[:, i:i + 1], axis=0),
                            in_=xn[:, i, :], in_offset=None).then_inc(s["scattered"], 16)
                pool.wait_ge(s["goals"], 1)
                for p in range(NP):
                    pool.wait_ge(s["ey_sb"], p + 1)
                    for c in range(2):
                        pool.indirect_dma_start(
                            out=token_y,
                            out_offset=bass.IndirectOffsetOnAxis(ap=goal[:, 2 * p + c:2 * p + c + 1], axis=0),
                            in_=ys[p % 2][:, c, :], in_offset=None).then_inc(s["y_out"][p % 2], 16)
                if f == 0:
                    attention_pool(pool)

        def attention_scalar(act, deviations):
            s = AS
            deviations(s, 0, 1, 1)
            act.wait_ge(s["mem"], 13)

            def turned():
                return banks[:, 1:3, :].rearrange("p a (g t) -> p (a g) t", g=4)

            def x_hi(i):
                act.wait_ge(s["xt_ps"], i + 1)
                nc.scalar.activation(xah[:], banks[:, 0, 0:D].rearrange("p (k t) -> p k t", k=KC), ACT.Copy)\
                    .then_inc(s["xt_hi"], 1)

            def qk_hi(i):
                act.wait_ge(s["qk_sb"], i + 1)
                nc.scalar.activation(stack[i % 3][:, :, :, 0:16], qk[:], ACT.Copy).then_inc(s["hi"], 1)
                nc.scalar.activation(stack[i % 3][:, 1, :, 16:32], qk[:, 1, :, :], ACT.Copy).then_inc(s["dup"], 1)
                nc.scalar.activation(stack[i % 3][:, 0, :, 32:48], qk[:, 0, :, :], ACT.Copy).then_inc(s["dup"], 1)

            def keep_k(i):
                b, j = divmod(i, TB)
                act.wait_ge(s["kt_ps"], i + 1)
                nc.scalar.activation(kT[b % 2][:, :, j * P:j * P + P], turned(), ACT.Copy).then_inc(s["kt_sb"], 1)

            def keep_q(i):
                act.wait_ge(s["qt_ps"], i + 1)
                if i < 4:
                    act.wait_ge(s["clear"], 2 * i + 2)
                nc.scalar.activation(qT[i % 4][0:64, 0:H:2, :], turned()[0:64], ACT.Copy).then_inc(s["q_even"], 1)

            def keep_maxima(i):
                act.wait_ge(s["mt_ps"], i + 1)
                if i >= 2:
                    act.wait_ge(s["m_in"][i % 2], 64 * (i // 2))
                nc.scalar.activation(mT[i % 2][:], banks[0:2 * H, 1, 0:P], ACT.Copy).then_inc(s["mt_sb"], 1)

            weighed = [4 * i + unit // (i % TB + 1) + 1 for i in range(NT) for unit in range(len(score_units(i)))]

            def exponentials(i, unit):
                u = score_base[i] + unit
                act.wait_ge(s["s2"], u + 1)
                if u >= NPR:
                    act.wait_ge(s["av"], weighed[u - NPR])
                nc.scalar.activation(prob[u % NPR], banks[:, 5 + u % 2, :], ACT.Exp, scale=HD ** -0.5)\
                    .then_inc(s["p"], 1)

            def keep_o(i):
                act.wait_ge(s["av"], 4 * (i + 1))
                nc.scalar.activation(oT[:], banks[:, 7, :].rearrange("p (g t) -> p g t", g=4), ACT.Copy)\
                    .then_inc(s["ot_ps_in"], 1)

            def o_hi(i):
                act.wait_ge(s["oc_ps"], i + 1)
                nc.scalar.activation(oh[:], banks[:, 0, 0:D].rearrange("p (k t) -> p k t", k=KC), ACT.Copy)\
                    .then_inc(s["oc_hi"], 1)

            after = {0: ((x_hi, 4),), 2: ((keep_maxima, 1), (keep_o, -1)), 4: ((keep_k, 3),), 7: ((keep_q, 3),),
                     8: ((o_hi, -1),), 14: ((qk_hi, 4),)}
            for i in range(-4, NT + 1):
                for step in range(16):
                    if 0 <= i < NT:
                        for unit in units_at(len(score_units(i)), step, 16):
                            exponentials(i, unit)
                    if (i, step) in ((-4, 2), (-1, 9)):
                        nth, a, b = (2, 1, TB) if i == -4 else (3, TB, NT)
                        deviations(s, a, b, nth)
                    if i == NT and step == 0:
                        deviations(FS[1], 0, NT - 2, 1)
                    for part, ahead in after.get(step, ()):
                        if 0 <= i + ahead < NT:
                            part(i + ahead)

        @block.scalar
        def _(act):
            def deviations(s, a, b, nth):
                act.wait_ge(s["var"], nth)
                nc.scalar.activation(rstd[:, a:b], ve[:, a:b], ACT.Sqrt).then_inc(s["sd"], 1)

            for f in range(2):
                s = FS[f]
                if f == 0:
                    deviations(s, 0, NT, 1)
                def norm_odd(q):
                    i = 2 * q + 1
                    nc.scalar.activation(xn[:, i, 0:D], x[:, i, :], ACT.Identity, bias=shift[:, i:i + 1],
                                         scale=rstd[:, i:i + 1]).then_inc(s["xn_odd"], 1)

                if f == 0:
                    piece_hi(0)
                act.wait_ge(s["xn"], 1)
                norm_odd(0)
                norm_odd(1)
                for q in range(NT // 2):
                    act.wait_ge(s["xt_ps"], q + 1)
                    nc.scalar.activation(xth[:, 2 * q:2 * q + 2, :, :], banks[:, q % 2, :]
                                         .rearrange("p (c k t) -> p c k t", c=2, k=KC), ACT.Copy).then_inc(s["xt_hi"], 1)
                    if q + 2 < NT // 2:
                        norm_odd(q + 2)
                    if f == 1 and q == 1:
                        deviations(s, NT - 2, NT, 2)
                    if f == 0 and q in (1, 3):
                        piece_hi(1 + q // 2)
                    for g in {3: (0,), 5: (1,), 7: (2, 3)}.get(q, ()):
                        act.wait_ge(s["lt_ps"], g + 1)
                        if g >= 2:
                            act.wait_ge(s["logits"], g - 1)
                        nc.scalar.activation(turned_logits[:, g % 2, :], banks[0:E, 6 + g % 2, :], ACT.Copy)\
                            .then_inc(s["lt_sb"], 1)
                for i in range(NT):
                    act.wait_ge(s["sgate"], i + 1)
                    if i == 0:
                        act.wait_ge(s["logits"], 4)
                    else:
                        act.wait_ge(s["shid"], i)
                    nc.scalar.activation(sg[:], banks[:, 3, 0:SF], ACT.Silu).then_inc(s["ssilu"], 1)
                    if i == 2:
                        act.wait_ge(s["sig_in"], 2)
                        for w, m in ((w1, "m1"), (w2, "m2")):
                            nc.scalar.activation(w[:], route[m][:], ACT.Sigmoid).then_inc(s["sig"], 1)
                    if f == 0 and i in (1, 3):
                        piece_hi(3 + i // 2)
                    if i in expert_split[f]:
                        piece_hi(N_RES + f * E + expert_split[f].index(i))
                    act.wait_ge(s["sht_ps"], i + 1)
                    if i >= 1:
                        act.wait_ge(s["sy"], i)
                    nc.scalar.activation(shh[:], banks[:, 5, 0:SC * P], ACT.Copy).then_inc(s["sht_hi"], 1)

                def silu(p):
                    act.wait_ge(s["egu"], p + 1)
                    nc.scalar.activation(eg[:], banks[:, 3:5, 0:FF], ACT.Silu).then_inc(s["esilu"], 1)

                def x_hi(p, par):
                    act.wait_ge(s["ext_ps"], p + 1)
                    nc.scalar.activation(exh[par][:], banks[:, 0, :].rearrange("p (c k t) -> p c k t", c=2, k=KC),
                                         ACT.Copy).then_inc(s["ext_hi"], 1)

                def h_hi(p):
                    act.wait_ge(s["eht_ps"], p + 1)
                    nc.scalar.activation(ehh[:], banks[:, 5, :].rearrange("p (c k t) -> p c k t", c=2, k=HC),
                                         ACT.Copy).then_inc(s["eht_hi"], 1)

                act.wait_ge(s["sy"], NT)
                x_hi(0, 0)
                with act.Fori(0, NP // 2 - 1) as m:
                    i = 2 * m
                    for par in range(2):
                        x_hi(i + par + 1, 1 - par)
                        silu(i + par)
                        h_hi(i + par)
                x_hi(NP - 1, 1)
                silu(NP - 2)
                h_hi(NP - 2)
                silu(NP - 1)
                h_hi(NP - 1)
                if f == 0:
                    attention_scalar(act, deviations)

        def attention_tensor(pe):
            s = AS

            def x_turn(i):
                pe.wait_ge(s["xn"], i + 1)
                if i >= 6:
                    pe.wait_ge(s["done"], i - 5)
                elif i >= 1:
                    pe.wait_ge(s["xt_lo"], i)
                for k in range(KC):
                    mm = pe.transpose(banks[:, 0, k * P:k * P + P], xa[i % 2][:, k * P:k * P + P], ident)
                mm.then_inc(s["xt_ps"], 1)

            def project(i, k, which):
                if k == 0 and which == 0:
                    pe.wait_ge(s["xt_lo"], i + 1)
                    if i == 0:
                        pe.wait_ge(split_res, N_RES)
                    if i >= 1:
                        pe.wait_ge(s["q_even"], i)
                        pe.wait_ge(s["q_odd"], i)
                at = W_QKV + k * 3 * D + which * 2 * D
                n = D if which else 2 * D
                mm = exact3(pe, banks[:, 1 + which, 0:n], xah[:, k, :], xal[:, k, :], wh[:, at:at + n],
                            wl[:, at:at + n], k == 0, k == KC - 1)
                if k == KC - 1 and which == 1:
                    mm.then_inc(s["qkv"], 1)

            def turn_stack(i, which, done):
                for g in range(H // 2):
                    mm = pe.matmul(banks[:, 1 + g // 4, (g % 4) * P:(g % 4) * P + P],
                                   stack[i % 3][:, which, 2 * g:2 * g + 2, :].rearrange("p a b -> p (a b)"),
                                   id_r[:], start=True, stop=True)
                mm.then_inc(s[done], 1)

            def k_turn(i):
                pe.wait_ge(s["v_sb"], i + 1)
                if i >= 2:
                    pe.wait_ge(s["mt_sb"], i - 1)
                pe.wait_ge(s["lo"], 2 * i + 2)
                pe.wait_ge(s["dup"], 2 * i + 2)
                turn_stack(i, 1, "kt_ps")

            def q_turn(i):
                pe.wait_ge(s["kt_sb"], i + 1)
                turn_stack(i, 0, "qt_ps")

            def m_turn(i):
                pe.wait_ge(s["m_hi"], 2 * i + 2)
                if i + 2 < NT:
                    pe.wait_ge(s["v_sb"], i + 3)
                elif i + 1 < NT:
                    pe.wait_ge(s["q_even"], i + 2)
                    pe.wait_ge(s["q_odd"], i + 2)
                else:
                    pe.wait_ge(s["mt_sb"], i)
                pe.matmul(banks[0:2 * H, 1, 0:P], m_neg[:].rearrange("p a b c -> p (a b c)"), id_r[:],
                          start=True, stop=True).then_inc(s["mt_ps"], 1)

            def bound(i, unit):
                b, j = divmod(i, TB)
                n = (j + 1) * P
                u = bound_base[i] + unit
                heads = bound_units(i)[unit]
                if unit == 0:
                    pe.wait_ge(s["q_even"], i + 1)
                    pe.wait_ge(s["q_odd"], i + 1)
                if u >= 2:
                    pe.wait_ge(s["mx"], u - 1)
                o = banks[:, 3 + u % 2, 0:len(heads) * n].rearrange("p (h s) -> p h s", s=n)
                for a, h in enumerate(heads):
                    mm = pe.matmul(o[:, a, :], qT[i % 4][:, h, :], kT[b % 2][:, h // 2, 0:n], start=True, stop=True)
                if len(heads) > 1:
                    mm = pe.matmul(o[:, :, n - P:n], id_bf[:], mask_bf[:].unsqueeze(1).to_broadcast([P, len(heads), P]),
                                   start=False, stop=True, skip_group_check=True)
                mm.then_inc(s["s1"], 1)

            def scores(i, unit):
                b, j = divmod(i, TB)
                u = score_base[i] + unit
                if unit == 0:
                    pe.wait_ge(s["m_in"][i % 2], 64 * (i // 2 + 1))
                if u >= 2:
                    pe.wait_ge(s["p"], u - 1)
                for a, (pair, t) in enumerate(score_units(i)[unit]):
                    o = banks[:, 5 + u % 2, a * 2 * P:(a + 1) * 2 * P].rearrange("p (h s) -> p h s", h=2)
                    mm = pe.matmul(o, kT[b % 2][:, pair, t * P:t * P + P], qT[i % 4][:, 2 * pair:2 * pair + 2, :],
                                   start=True, stop=True)
                mm.then_inc(s["s2"], 1)

            def weigh(i, g):
                b, j = divmod(i, TB)
                pe.wait_ge(s["p"], score_base[i] + (g + 1) * (j + 1))
                pe.wait_ge(s["causal"], 8 * i + 2 * g + 2)
                if g == 0 and i >= 1:
                    pe.wait_ge(s["ot_ps_in"], i)
                for t in range(j + 1):
                    for c in range(4):
                        h = 4 * g + c
                        unit, half = divmod(h // 2 * (j + 1) + t, 2)
                        at = (2 * half + h % 2) * P
                        mm = pe.matmul(banks[32 * c:32 * c + 32, 7, g * P:g * P + P], v[b % 2][:, t, h, :],
                                       prob[(score_base[i] + unit) % NPR][:, at:at + P], start=t == 0, stop=t == j)
                mm.then_inc(s["av"], 1)

            def o_turn(i):
                pe.wait_ge(s["ot_ps_in"], i + 1)
                if i + 5 < NT:
                    pe.wait_ge(s["xt_lo"], i + 6)
                else:
                    pe.wait_ge(s["done"], i)
                for g in range(4):
                    mm = pe.transpose(banks[:, 0, g * P:g * P + P], oT[:, g, :], ident)
                mm.then_inc(s["o_ps"], 1)

            def oc_turn(i):
                pe.wait_ge(s["o_sb"], i + 1)
                for k in range(KC):
                    mm = pe.transpose(banks[:, 0, k * P:k * P + P],
                                      ot[:].rearrange("p h d -> p (h d)")[:, k * P:k * P + P], ident)
                mm.then_inc(s["oc_ps"], 1)

            def out_project(i):
                pe.wait_ge(s["oc_lo"], i + 1)
                for k in range(KC):
                    at = W_O + k * D
                    mm = exact3(pe, banks[:, 0, 0:D], oh[:, k, :], ol[:, k, :], wh[:, at:at + D], wl[:, at:at + D],
                                k == 0, k == KC - 1)
                mm.then_inc(s["y"], 1)

            before = {0: ((x_turn, 4),), 2: ((m_turn, 1),), 4: ((k_turn, 3),), 5: ((o_turn, -1),), 7: ((q_turn, 3),),
                      8: ((oc_turn, -1),), 10: ((project, 4, 0, 0),), 11: ((project, 4, 1, 0),),
                      12: ((out_project, -1), (project, 4, 0, 1)), 13: ((project, 4, 1, 1),)}
            for i in range(-4, NT + 1):
                for step in range(16):
                    for part, ahead, *piece in before.get(step, ()):
                        if 0 <= i + ahead < NT:
                            part(i + ahead, *piece)
                    if 0 <= i < NT:
                        for unit in units_at(len(score_units(i)), step, 16):
                            scores(i, unit)
                    if 0 <= i + 2 < NT:
                        for unit in units_at(len(bound_units(i + 2)), step, 16):
                            bound(i + 2, unit)
                    if step == 2 and 0 <= i - 1 < NT:
                        weigh(i - 1, 3)
                    if step in (5, 9, 13) and 0 <= i < NT:
                        weigh(i, (step - 5) // 4)

        @block.tensor
        def _(pe):
            pe.wait_ge(cst_in, 16)
            for f in range(2):
                s = FS[f]
                logits = banks[:, 2, 0:NT * E].rearrange("p (i e) -> p i e", e=E)

                def x_turns(q):
                    pe.wait_ge(s["xn"], q + 1)
                    pe.wait_ge(s["xn_odd"], q + 1)
                    if q >= 2:
                        pe.wait_ge(s["xt_lo"], q - 1)
                    for c in range(2):
                        for k in range(KC):
                            at = (c * KC + k) * P
                            mm = pe.transpose(banks[:, q % 2, at:at + P], xn[:, 2 * q + c, k * P:k * P + P], ident)
                    mm.then_inc(s["xt_ps"], 1)

                def router(g):
                    pe.wait_ge(s["xt_lo"], 2 * g + 2)
                    if g == 0:
                        pe.wait_ge(split_res, 1)
                    if g >= 2:
                        pe.wait_ge(s["lt_sb"], g - 1)
                    o = banks[0:E, 6 + g % 2, :].rearrange("p (c t) -> p c t", c=4)
                    for k in range(KC):
                        w = slice(W_GATE + k * E, W_GATE + k * E + E)
                        mm = exact3(pe, o, wh[:, w], wl[:, w], xth[:, 4 * g:4 * g + 4, k, :],
                                    xtl[:, 4 * g:4 * g + 4, k, :], k == 0, k == KC - 1)
                    mm.then_inc(s["lt_ps"], 1)

                def logit_turns(g):
                    pe.wait_ge(s["lt_sb"], g + 1)
                    for c in range(4):
                        mm = pe.transpose(logits[:, 4 * g + c, :], turned_logits[:, g % 2, c * P:c * P + P],
                                          ident[0:E, 0:E])
                    mm.then_inc(s["logits"], 1)

                for q in range(4):
                    x_turns(q)
                router(0)
                for q in range(4, NT // 2):
                    x_turns(q)
                    if q % 2 == 1:
                        router(q // 2 - 1)
                        logit_turns(q // 2 - 2)
                router(3)
                logit_turns(2)
                logit_turns(3)

                def s_up(i):
                    if i == 0:
                        pe.wait_ge(split_res, 2)
                    else:
                        pe.wait_ge(s["shid"], i)
                    for half, done in ((0, "sgate"), (1, "sup")):
                        for k in range(KC):
                            at = W_SGU + (k * 2 + half) * SF
                            mm = exact3(pe, banks[:, 3 + half, 0:SF], xth[:, i, k, :], xtl[:, i, k, :],
                                        wh[:, at:at + SF], wl[:, at:at + SF], k == 0, k == KC - 1)
                        mm.then_inc(s[done], 1)

                def s_turn(i):
                    pe.wait_ge(s["shid"], i + 1)
                    if i >= 1:
                        pe.wait_ge(s["sht_lo"], i)
                    for c in range(SC):
                        mm = pe.transpose(banks[:, 5, c * P:c * P + P], sh[:, c * P:c * P + P], ident)
                    mm.then_inc(s["sht_ps"], 1)

                def s_down(i):
                    pe.wait_ge(s["sht_lo"], i + 1)
                    if i == 0:
                        pe.wait_ge(split_res, 3)
                        pe.wait_ge(s["lt_sb"], 4)
                    if i >= 2:
                        pe.wait_ge(s["sx"], i - 1)
                    for c in range(SC):
                        at = W_SD + c * D
                        mm = exact3(pe, banks[:, 6 + i % 2, 0:D], shh[:, c * P:c * P + P], shl[:, c * P:c * P + P],
                                    wh[:, at:at + D], wl[:, at:at + D], c == 0, c == SC - 1)
                    mm.then_inc(s["sy"], 1)

                def find_ranks():
                    pe.wait_ge(cst_bf, 5)
                    pe.wait_ge(s["picks"], 1)
                    ranks = banks[:, 2, 0:(NT + 1) * E].rearrange("p (i e) -> p i e", e=E)
                    pe.matmul(ranks, tri_bf[:], pick_bf[:], start=True, stop=False)
                    for i in range(NT):
                        mm = pe.matmul(ranks[:, i + 1:NT + 1, :], one_bf[:],
                                       pick_bf[:, i:i + 1, :].to_broadcast([P, NT - i, E]),
                                       start=False, stop=i == NT - 1)
                    mm.then_inc(s["ranks"], 1)

                s_up(0)
                s_turn(0)
                for i in range(1, NT):
                    s_up(i)
                    s_down(i - 1)
                    if i == 3:
                        find_ranks()
                    s_turn(i)
                eh2 = eh[:].rearrange("p e w -> p (e w)")
                el2 = el[:].rearrange("p e w -> p (e w)")

                def experts_of(p):
                    _, at = nc.values_load_multi_w_load_instructions(
                        tile_weights[0:1, 2 * p:2 * p + 4], engines=[mybir.EngineType.PE], min_val=0,
                        max_val=(E - 1) * EW, skip_runtime_bounds_check_because="the table holds expert offsets below the row length")
                    return at

                def turn(p):
                    n = p % 4
                    pe.wait_ge(s["xs_in"][n], (p // 4 + 1) * 16)
                    if p >= 1:
                        pe.wait_ge(s["ext_lo"], p)
                    for c in range(2):
                        for k in range(KC):
                            at = (c * KC + k) * P
                            mm = pe.transpose(banks[:, 0, at:at + P], xs[n][:, c, k * P:k * P + P], ident)
                    mm.then_inc(s["ext_ps"], 1)

                def up(p, par, which):
                    pe.wait_ge(s["ext_lo"], p + 1)
                    for c in range(2):
                        e = which[c]
                        for k in range(KC):
                            w, n = k * 2 * FF, 2 * FF
                            mm = exact3(pe, banks[:, 3 + c, 0:2 * FF], exh[par][:, c, k, :], exl[par][:, c, k, :],
                                        eh2[:, bass.ds(e + w, n)], el2[:, bass.ds(e + w, n)], k == 0, k == KC - 1)
                    mm.then_inc(s["egu"], 1)

                def h_turn(p):
                    pe.wait_ge(s["ehid"], p + 1)
                    for c in range(2):
                        for k in range(HC):
                            at = (c * HC + k) * P
                            mm = pe.transpose(banks[:, 5, at:at + P], ehid[:, c, k * P:k * P + P], ident)
                    mm.then_inc(s["eht_ps"], 1)

                def down(p, par, which):
                    pe.wait_ge(s["eht_lo"], p + 1)
                    for c in range(2):
                        e = which[c]
                        for k in range(HC):
                            w, n = EW_D + k * D, D
                            mm = exact3(pe, banks[:, 6 + par, c * D:(c + 1) * D], ehh[:, c, k, :], ehl[:, c, k, :],
                                        eh2[:, bass.ds(e + w, n)], el2[:, bass.ds(e + w, n)], k == 0, k == HC - 1)
                    mm.then_inc(s["ey"], 1)

                s_down(NT - 1)
                turn(0)
                pe.wait_ge(split_exp, 2 * (f + 1) * E)
                pe.wait_ge(s["slots"], 3)
                regs = {}
                for p in range(NP):
                    if p % 2 == 0:
                        four = experts_of(p)
                        regs[p], regs[p + 1] = four[0:2], four[2:4]
                    if p + 1 < NP:
                        turn(p + 1)
                    up(p, p % 2, regs[p])
                    if p >= 1:
                        down(p - 1, (p - 1) % 2, regs[p - 1])
                    h_turn(p)
                down(NP - 1, 1, regs[NP - 1])
                if f == 0:
                    attention_tensor(pe)

        def attention_vector(dve, link, norm_stats, norm_factors, combine):
            s = AS
            combine(FS[0], 0, 1, True)
            norm_factors(s, 0, 1, 1)
            dve.wait_ge(bias_in, 32)
            dve.wait_ge(s["mem"], 13)

            def keep_q(i):
                dve.wait_ge(s["qt_ps"], i + 1)
                if i < 4:
                    dve.wait_ge(s["clear"], 2 * i + 2)
                nc.vector.tensor_copy(qT[i % 4][64:128, 1:H:2, :], turned(64, 128)).then_inc(s["q_odd"], 1)

            def turned(a, b):
                return banks[a:b, 1:3, :].rearrange("p a (g t) -> p (a g) t", g=4)

            def x_lo(i):
                dve.wait_ge(s["xt_hi"], i + 1)
                nc.vector.tensor_tensor(xal[:], banks[:, 0, 0:D].rearrange("p (k t) -> p k t", k=KC),
                                        xah[:].bitcast(F32), ALU.subtract).then_inc(s["xt_lo"], 1)

            def add_bias(i):
                b, j = divmod(i, TB)
                dve.wait_ge(s["qkv"], i + 1)
                if i >= 1:
                    dve.wait_ge(s["lo"], 2 * i)
                    dve.wait_ge(s["dup"], 2 * i)
                nc.vector.tensor_tensor(qk[:], banks[:, 1, :].rearrange("p (a h d) -> p a h d", a=2, h=H),
                                        bqkv[:, 0:2 * D].rearrange("p (a h d) -> p a h d", a=2, h=H), ALU.add)\
                    .then_inc(s["qk_sb"], 1)
                nc.vector.tensor_tensor(v[b % 2][:, j, :, 0:HD], banks[:, 2, 0:D].rearrange("p (h d) -> p h d", h=H),
                                        bqkv[:, 2 * D:3 * D].rearrange("p (h d) -> p h d", h=H), ALU.add)\
                    .then_inc(s["v_sb"], 1)

            def maximum(i, unit):
                n = (i % TB + 1) * P
                u = bound_base[i] + unit
                heads = bound_units(i)[unit]
                dve.wait_ge(s["s1"], u + 1)
                if unit == 0 and i >= 2:
                    dve.wait_ge(s["m_hi"], 2 * i - 2)
                if len(heads) == 1:
                    dve.wait_ge(s["mx"], u - 1)
                    nc.vector.tensor_tensor_reduce(masked[u % 2][:, 0:n], banks[:, 3 + u % 2, 0:n], mask_row[:, S - n:S],
                                                   1.0, -3e38, ALU.add, ALU.max,
                                                   smax[i % 2][:, heads[0]:heads[0] + 1]).then_inc(s["mx"], 1)
                    return
                nc.vector.tensor_reduce(smax[i % 2][:, heads[0]:heads[-1] + 1],
                                        banks[:, 3 + u % 2, 0:len(heads) * n].rearrange("p (h s) -> p h s", s=n),
                                        X, ALU.max).then_inc(s["mx"], 1)

            def put_maxima(i):
                dve.wait_ge(s["mx"], bound_base[i + 1])
                if i >= 1:
                    dve.wait_ge(s["mt_ps"], i)
                m = smax[i % 2][:].rearrange("p (g o) -> p o g", o=2)
                nc.vector.tensor_scalar(m_neg[:, :, 0, :], m, -1.0, None, ALU.mult).then_inc(s["m_hi"], 1)
                dve.wait_ge(s["m_hi"], 2 * i + 1)
                nc.vector.scalar_tensor_tensor(m_neg[:, :, 1, :], m, -1.0, m_neg[:, :, 0, :].bitcast(F32),
                                               ALU.mult, ALU.subtract).then_inc(s["m_hi"], 1)

            def divide(i):
                dve.wait_ge(s["o_ps"], i + 1)
                o = banks[:, 0, :].rearrange("p (h c) -> p h c", c=32)
                link(nc.vector.reciprocal(rden[:], o[:, :, 16]))
                nc.vector.tensor_tensor(ot[:], o[:, :, 0:HD], rden[:].unsqueeze(2).to_broadcast([P, H, HD]), ALU.mult)\
                    .then_inc(s["o_sb"], 1)

            def o_lo(i):
                dve.wait_ge(s["oc_hi"], i + 1)
                nc.vector.tensor_tensor(ol[:], banks[:, 0, 0:D].rearrange("p (k t) -> p k t", k=KC),
                                        oh[:].bitcast(F32), ALU.subtract).then_inc(s["oc_lo"], 1)

            def residual(i):
                dve.wait_ge(s["y"], i + 1)
                dve.wait_ge(s["bo"], i + 1)
                nc.vector.tensor_tensor(x[:, i, :], banks[:, 0, 0:D], x[:, i, :], ALU.add).then_inc(s["done"], 1)

            def row_stats(i):
                dve.wait_ge(s["done"], i + 1)
                norm_stats(i)

            after = {1: ((x_lo, 4),), 3: ((row_stats, -2),), 5: ((divide, -1),), 7: ((keep_q, 3),), 9: ((o_lo, -1),),
                     12: ((residual, -1),), 13: ((add_bias, 4),), 15: ((put_maxima, 2),)}
            for i in range(-4, NT + 1):
                for step in range(16):
                    if i == -4 and step == 2:
                        combine(FS[0], 1, TB, True)
                        norm_factors(s, 1, TB, 2)
                        nc.vector.memset(mask_row[:, 0:S - P], 0.0)
                        nc.vector.tensor_copy(mask_row[:, S - P:S], cst[:, C_MASK:C_MASK + P])
                    if -4 < i < 0 and step in (3, 8):
                        half = TB * (i + 4) + (0 if step == 3 else 2)
                        combine(FS[0], half, half + 2, True)
                    if i == -1 and step == 9:
                        norm_factors(s, TB, NT, 3)
                    if i == NT and step == 0:
                        norm_factors(FS[1], 0, NT - 2, 1)
                    if 0 <= i + 2 < NT:
                        for unit in units_at(len(bound_units(i + 2)), step, 16):
                            maximum(i + 2, unit)
                    for part, ahead in after.get(step, ()):
                        if 0 <= i + ahead < NT:
                            part(i + ahead)
            dve.wait_ge(s["done"], NT)
            row_stats(NT - 1)

        @block.vector
        def _(dve):
            def link(ins):
                links[0] += 1
                ins.then_inc(chain, 1)
                dve.wait_ge(chain, links[0])

            def norm_stats(i):
                nc.vector.bn_stats(stats[:, i, :], x[:, i, :]).then_inc(row_stats_in, 1)

            def norm_factors(s, a=0, b=NT, nth=1):
                norms[0] += b - a
                dve.wait_ge(row_stats_in, norms[0])
                for i in range(a, b):
                    ins = nc.vector.bn_aggr(mv[:, i, :], stats[:, i, :])
                link(ins)
                nc.vector.tensor_scalar(ve[:, a:b], mv[:, a:b, 1], EPS, None, ALU.add).then_inc(s["var"], 1)
                dve.wait_ge(s["sd"], nth)
                link(nc.vector.reciprocal(rstd[:, a:b], rstd[:, a:b]))
                link(nc.vector.tensor_tensor(nt1[:, a:b], ve[:, a:b], rstd[:, a:b], ALU.mult))
                link(nc.vector.tensor_tensor(nt2[:, a:b], nt1[:, a:b], rstd[:, a:b], ALU.mult))
                link(nc.vector.tensor_scalar(nt1[:, a:b], nt2[:, a:b], -0.5, 1.5, ALU.mult, ALU.add))
                if s is AS:
                    nc.vector.tensor_tensor(rstd[:, a:b], rstd[:, a:b], nt1[:, a:b], ALU.mult).then_inc(s["rstd"], 1)
                else:
                    link(nc.vector.tensor_tensor(rstd[:, a:b], rstd[:, a:b], nt1[:, a:b], ALU.mult))
                    nc.vector.scalar_tensor_tensor(shift[:, a:b], mv[:, a:b, 0], -1.0, rstd[:, a:b], ALU.mult, ALU.mult)

            def combine(s, a, b, with_stats):
                g = a // 4
                ways = len(s["pick_in"])
                dve.wait_ge(s["pick_in"][g % ways], 32 * (g // ways + 1))
                for i in range(a, b):
                    c = i % 4
                    nc.vector.scalar_tensor_tensor(x[:, i, :], picks_of(g, f)[0][:, c, :], w1[:, i:i + 1], x[:, i, :],
                                                   ALU.mult, ALU.add).then_inc(chain, 1)
                for i in range(a, b):
                    c = i % 4
                    links[0] += 1
                    dve.wait_ge(chain, links[0])
                    nc.vector.scalar_tensor_tensor(x[:, i, :], picks_of(g, f)[1][:, c, :], w2[:, i:i + 1], x[:, i, :],
                                                   ALU.mult, ALU.add).then_inc(s["combined"], 1)
                if with_stats:
                    for i in range(a, b):
                        dve.wait_ge(s["combined"], i + 1)
                        norm_stats(i)

            norms = [0]
            for i in range(NT):
                if i % TB == 0:
                    dve.wait_ge(x_in_s[i // TB], 16)
                norm_stats(i)
            for f in range(2):
                s = FS[f]
                r = route
                if f == 0:
                    norm_factors(s)
                if f == 0:
                    dve.wait_ge(cst_in, 16)
                    for dst, at in ((tri_bf, C_U), (one_bf, C_ONE), (id_bf, C_ID), (mask_bf, C_MASK), (id_r, C_ID)):
                        nc.vector.tensor_copy(dst[:], cst[:, at:at + P]).then_inc(cst_bf, 1)
                nc.vector.tensor_copy(xn[:, :, D], cst[:, C_TOKEN:C_TOKEN + NT])
                for q in range(NT // 2 + 1):
                    if q < NT // 2:
                        i = 2 * q
                        nc.vector.tensor_scalar(xn[:, i, 0:D], x[:, i, :], mv[:, i, 0:1], rstd[:, i:i + 1],
                                                ALU.subtract, ALU.mult).then_inc(s["xn"], 1)
                    if f == 1 and q == 2:
                        norm_factors(s, NT - 2, NT, 2)
                    if q >= 1:
                        p = q - 1
                        dve.wait_ge(s["xt_hi"], p + 1)
                        nc.vector.tensor_tensor(xtl[:, 2 * p:2 * p + 2, :, :],
                                                banks[:, p % 2, :].rearrange("p (c k t) -> p c k t", c=2, k=KC),
                                                xth[:, 2 * p:2 * p + 2, :, :].bitcast(F32), ALU.subtract)\
                            .then_inc(s["xt_lo"], 1)
                iota = cst[:, C_IOTA:C_IOTA + NT * E].rearrange("p (i e) -> p i e", e=E)

                def wide(ap):
                    return ap[:].unsqueeze(2).to_broadcast([P, NT, E])

                def largest(m):
                    nc.vector.tensor_reduce(r[m][:], r["lg"][:], X, ALU.max).then_inc(s["sig_in"], 1)

                def first_logits():
                    link(nc.vector.tensor_copy(r["lg"][:], banks[:, 2, 0:NT * E].rearrange("p (i e) -> p i e", e=E)))
                    largest("m1")

                def first_place(m):
                    dve.wait_ge(s["sig_in"], 1 if m == "m1" else 2)
                    link(nc.vector.tensor_tensor(r["c"][:], r["lg"][:], wide(r[m]), ALU.is_equal))
                    link(nc.vector.scalar_tensor_tensor(r["c"][:], r["c"][:], -float(E), iota, ALU.mult, ALU.add))
                    link(nc.vector.tensor_reduce(r["i1"][:], r["c"][:], X, ALU.min))

                def one_hot(hot):
                    link(nc.vector.tensor_scalar(r["i1"][:], r["i1"][:], float(E), None, ALU.add))
                    link(nc.vector.tensor_tensor(r[hot][:], iota, wide(r["i1"]), ALU.is_equal))

                def mark_first():
                    one_hot("oh1")
                    nc.vector.tensor_copy(xn[:, :, D + 1], r["i1"][:])

                def second_logits():
                    link(nc.vector.scalar_tensor_tensor(r["lg"][:], r["oh1"][:], -BIG, r["lg"][:], ALU.mult, ALU.add))
                    largest("m2")

                def mark_both():
                    one_hot("oh2")
                    nc.vector.tensor_tensor(pick_bf[:, 0:NT, :], r["oh1"][:], r["oh2"][:], ALU.add)\
                        .then_inc(s["picks"], 1)

                def pick_weights():
                    dve.wait_ge(s["sig"], 2)
                    link(nc.vector.scalar_tensor_tensor(r["den"][:], w1[:], 1e-20, w2[:], ALU.add, ALU.add))
                    link(nc.vector.reciprocal(r["den"][:], r["den"][:]))
                    for w in (w1, w2):
                        link(nc.vector.scalar_tensor_tensor(w[:], w[:], 1.25, r["den"][:], ALU.mult, ALU.mult))

                def count_tiles():
                    dve.wait_ge(s["ranks"], 1)
                    link(nc.vector.tensor_copy(r["rk"][:], banks[:, 2, 0:(NT + 1) * E].rearrange("p (i e) -> p i e", e=E)))
                    link(nc.vector.tensor_tensor(r["cnt"][:], r["rk"][:, NT, :].unsqueeze(2).to_broadcast([P, E, NT]),
                                                 cst[:, C_THR:C_THR + E * NT].rearrange("p (e j) -> p e j", e=E), ALU.is_gt))
                    link(nc.vector.tensor_reduce(r["te"][:], r["cnt"][:], X, ALU.add))

                def first_rows():
                    link(nc.vector.tensor_tensor(r["ee"][:], cst[:, C_TRI:C_TRI + E * E].rearrange("p (a b) -> p a b", a=E),
                                                 r["te"][:].unsqueeze(1).to_broadcast([P, E, E]), ALU.mult))
                    link(nc.vector.tensor_reduce(r["inc"][:], r["ee"][:], X, ALU.add))
                    link(nc.vector.tensor_tensor(r["te"][:], r["inc"][:], r["te"][:], ALU.subtract))
                    link(nc.vector.scalar_tensor_tensor(r["rk"][:, 0:NT, :],
                                                        r["te"][:].unsqueeze(1).to_broadcast([P, NT, E]),
                                                        float(P), r["rk"][:, 0:NT, :], ALU.mult, ALU.add))

                def pick_slots(hot, sl, slot):
                    link(nc.vector.tensor_tensor(r["c"][:], r[hot][:], r["rk"][:, 0:NT, :], ALU.mult))
                    link(nc.vector.tensor_reduce(r[sl][:], r["c"][:], X, ALU.add))
                    nc.vector.tensor_copy(slot[:], r[sl][:]).then_inc(s["slots"], 1)

                def first_slots():
                    first_rows()
                    pick_slots("oh1", "sl1", slot1)

                def tile_offsets():
                    link(nc.vector.tensor_tensor(r["tb"][:], r["inc"][:].unsqueeze(1).to_broadcast([P, 2 * NP, E]),
                                                 cst[:, C_J:C_J + 2 * NP * E].rearrange("p (j e) -> p j e", e=E),
                                                 ALU.is_le))
                    link(nc.vector.tensor_reduce(r["tf"][:], r["tb"][:], X, ALU.add))
                    link(nc.vector.tensor_scalar(r["to"][:], r["tf"][0:1, :], float(E - 1), float(EW), ALU.min, ALU.mult))
                    nc.vector.tensor_copy(tile_weights[:], r["to"][:]).then_inc(s["slots"], 1)

                def s_out(i):
                    dve.wait_ge(s["sy"], i + 1)
                    nc.vector.scalar_tensor_tensor(x[:, i, :], banks[:, 6 + i % 2, 0:D], 0.5, x[:, i, :],
                                                   ALU.mult, ALU.add).then_inc(s["sx"], 1)

                def split_piece(n, part):
                    if (n - N_RES) % E == POOL_PIECES[f] > 0 and part == 0:
                        dve.wait_ge(split_exp, 2 * (n - N_RES))
                    dve.wait_ge(split_hi, n + 1)
                    piece_lo(nc.vector, n, part, 2)

                dve.wait_ge(s["logits"], 4)
                nc.vector.memset(sh[:, SF:SC * P], 0.0)
                nc.vector.memset(pick_bf[:, NT, :], 0.0)
                routing = {0: ((first_logits,), (first_place, "m1")), 1: ((mark_first,), (second_logits,)),
                           2: ((first_place, "m2"), (mark_both,)), 3: ((count_tiles,), (first_slots,)),
                           4: ((pick_slots, "oh2", "sl2", slot2), (tile_offsets,)),
                           6: ((pick_weights,), None)}
                for e in range(POOL_PIECES[f], E):
                    n = N_RES + f * E + e
                    routing[expert_split[f][e]] = ((split_piece, n, 0), (split_piece, n, 1))
                for i in range(NT):
                    dve.wait_ge(s["ssilu"], i + 1)
                    dve.wait_ge(s["sup"], i + 1)
                    if i >= 1:
                        dve.wait_ge(s["sht_ps"], i)
                    nc.vector.tensor_tensor(sh[:, 0:SF], sg[:], banks[:, 4, 0:SF], ALU.mult).then_inc(s["shid"], 1)
                    if i >= 1:
                        s_out(i - 1)
                    before_lo, after_lo = routing.get(i, (None, None))
                    if before_lo:
                        before_lo[0](*before_lo[1:])
                    dve.wait_ge(s["sht_hi"], i + 1)
                    nc.vector.tensor_tensor(shl[:], banks[:, 5, 0:SC * P], shh[:].bitcast(F32), ALU.subtract)\
                        .then_inc(s["sht_lo"], 1)
                    if after_lo:
                        after_lo[0](*after_lo[1:])
                s_out(NT - 1)

                link(nc.vector.memset(ehid[:], 0.0))

                def x_lo(p, par):
                    dve.wait_ge(s["ext_hi"], p + 1)
                    nc.vector.tensor_tensor(exl[par][:], banks[:, 0, :].rearrange("p (c k t) -> p c k t", c=2, k=KC),
                                            exh[par][:].bitcast(F32), ALU.subtract).then_inc(s["ext_lo"], 1)

                def hidden(p):
                    dve.wait_ge(s["esilu"], p + 1)
                    nc.vector.tensor_tensor(ehid[:, :, 0:FF], eg[:], banks[:, 3:5, FF:2 * FF], ALU.mult)\
                        .then_inc(s["ehid"], 1)

                def h_lo(p):
                    dve.wait_ge(s["eht_hi"], p + 1)
                    nc.vector.tensor_tensor(ehl[:], banks[:, 5, :].rearrange("p (c k t) -> p c k t", c=2, k=HC),
                                            ehh[:].bitcast(F32), ALU.subtract).then_inc(s["eht_lo"], 1)

                def y_out(p, par, stores):
                    dve.wait_ge(s["ey"], p + 1)
                    if stores is not None:
                        dve.wait_ge(s["y_out"][par], stores * 32)
                    nc.vector.tensor_copy(ys[par][:], banks[:, 6 + par, :].rearrange("p (c d) -> p c d", c=2))\
                        .then_inc(s["ey_sb"], 1)

                x_lo(0, 0)
                x_lo(1, 1)
                dve.wait_ge(s["marks_in"], 16)
                nc.vector.tensor_tensor(r["same"][:], marks[:, :, 1], r["tf"][:], ALU.is_equal)
                nc.vector.tensor_scalar(r["fill"][:], marks[:, :, 1], 0.0, None, ALU.is_lt)
                link(nc.vector.tensor_scalar(r["goal"][:], marks[:, :, 0], 0.0, None, ALU.add))
                link(nc.vector.scalar_tensor_tensor(r["goal"][:], r["same"][:], -float(T), r["goal"][:],
                                                    ALU.mult, ALU.add))
                link(nc.vector.tensor_tensor(r["fill"][:], r["fill"][:], cst[:, C_TILE:C_TILE + 2 * NP], ALU.mult))
                link(nc.vector.tensor_tensor(r["goal"][:], r["goal"][:], r["fill"][:], ALU.add))
                nc.vector.tensor_copy(goal[:], r["goal"][:]).then_inc(s["goals"], 1)

                hidden(0)
                h_lo(0)
                x_lo(2, 0)
                hidden(1)
                y_out(0, 0, None)
                h_lo(1)
                x_lo(3, 1)
                hidden(2)
                y_out(1, 1, None)
                h_lo(2)
                with dve.Fori(0, NP // 2 - 2) as m:
                    i = 2 * m + 3
                    for d, par in ((0, 1), (1, 0)):
                        x_lo(i + d + 1, 1 - par)
                        hidden(i + d)
                        y_out(i + d - 1, 1 - par, m + 1)
                        h_lo(i + d)
                hidden(NP - 1)
                y_out(NP - 2, 0, NP // 2 - 1)
                h_lo(NP - 1)
                y_out(NP - 1, 1, NP // 2 - 1)
                if f == 0:
                    attention_vector(dve, link, norm_stats, norm_factors, combine)
                else:
                    for g in range(B):
                        combine(s, 4 * g, 4 * g + 4, False)


def constants():
    c = np.zeros((P, C_END), np.float32)
    r = np.arange(P)
    c[:, C_ID:C_ID + P] = np.eye(P)
    c[:, C_U:C_U + P] = r[:, None] < r[None, :]
    c[:, C_ONE:C_ONE + P] = 1.0
    c[:, C_MASK:C_MASK + P] = np.where(r[None, :] > r[:, None], -BIG, 0.0)
    c[:, C_IOTA:C_IOTA + NT * E] = np.tile(np.arange(E), NT)
    c[:, C_THR:C_THR + E * NT] = np.tile(P * np.arange(NT), E)
    c[:, C_TRI:C_TRI + E * E] = (np.arange(E)[None, :] <= np.arange(E)[:, None]).reshape(-1)
    c[:, C_J:C_J + 2 * NP * E] = np.repeat(np.arange(2 * NP), E)
    c[:, C_TOKEN:C_TOKEN + NT] = T + P * np.arange(NT)[None, :] + r[:, None]
    c[:, C_TILE:C_TILE + 2 * NP] = P * np.arange(2 * NP)
    return c


def rows_by_chunk(w):
    k = w.shape[0] // P
    return w.reshape(k, P, -1).transpose(1, 0, 2).reshape(P, -1)


def padded(w, rows):
    return np.concatenate([w, np.zeros((rows - w.shape[0], w.shape[1]), w.dtype)])


def kernel(**inputs):
    import concourse.bacc as bacc
    from concourse.bass_utils import run_bass_kernel_spmd as run

    a = {k.replace("L0_", ""): np.asarray(v) for k, v in inputs.items()}
    resident = np.concatenate([
        rows_by_chunk(a["ffn_gate_w"].T),
        rows_by_chunk(np.concatenate([a["ffn_shared_wg"], a["ffn_shared_wu"]]).T),
        rows_by_chunk(padded(a["ffn_shared_wd"].T, SC * P)),
        rows_by_chunk(a["attn_Wqkv"]),
        rows_by_chunk(a["attn_Wo"])], axis=1)
    experts = np.stack([np.concatenate([
        rows_by_chunk(np.concatenate([a["ffn_exp_wg"][e], a["ffn_exp_wu"][e]]).T),
        rows_by_chunk(padded(a["ffn_exp_wd"][e].T, HC * P))], axis=1) for e in range(E)], axis=1)
    arrays = {
        "x_in": a["attn_x"], "w_res": resident, "w_exp": experts,
        "bias_qkv": np.broadcast_to(a["attn_bqkv"], (P, 3 * D)), "bias_o": np.broadcast_to(a["attn_bo"], (P, D)),
        "consts": constants()}
    arrays = {k: np.ascontiguousarray(v) for k, v in arrays.items()}
    nc = bacc.Bacc("TRN2", target_bir_lowering=False, num_devices=1)
    aps = [nc.dram_tensor(k, v.shape, F32, kind="ExternalInput").ap() for k, v in arrays.items()]
    out = nc.dram_tensor("out", (B, S, D), F32, kind="ExternalOutput").ap()
    build(nc, *aps, out)
    return run(nc, [arrays], core_ids=[0]).results[0]["out"]
```
